# Optimizing a Trainium2 kernel written in Bass

```python
import numpy as np
import jax
import jax.numpy as jnp

def _softmax(x, axis=-1):
    return jax.nn.softmax(x, axis=axis)

def _gelu(x):
    return jax.nn.gelu(x, approximate=True)

def _silu(x):
    return jax.nn.silu(x)

def _sigmoid(x):
    return jax.nn.sigmoid(x)

def _layernorm(x, axis=-1, eps=1e-05):
    m = jnp.mean(x, axis=axis, keepdims=True)
    v = jnp.var(x, axis=axis, keepdims=True)
    return (x - m) / jnp.sqrt(v + eps)

def _scatter_add(tgt, idx, src, axis=0):
    return tgt.at[idx].add(src)

def _segment_sum(src, seg, n):
    return jax.ops.segment_sum(src, seg, n)
kernel_name = 'mk_decoder_postln_d1_seqx_r8_240588'

def setup_inputs(seed: int=0):
    np.random.seed(seed)
    _w = jnp.asarray

    def _rec_inputs():
        import jax
        import jax.numpy as jnp
        _rk = jax.random.key(seed)
        x = -0.000125 + 0.9999 * jax.random.normal(jax.random.fold_in(_rk, 1), (4, 256, 256), jnp.float32)
        _lenS = 256 - jax.random.randint(jax.random.fold_in(_rk, 7), (4,), 0, max(1, 256 // 4) + 1, jnp.int32)
        _lenS2 = 256 - jax.random.randint(jax.random.fold_in(_rk, 8), (4,), 0, max(1, 256 // 4) + 1, jnp.int32)
        itok_BxS_13_99985 = jax.random.randint(jax.random.fold_in(_rk, 11), (4, 256), 13, 99986, jnp.int32)
        _ctx_2048P = jax.random.normal(jax.random.fold_in(_rk, 12), (4, 16, 256), jnp.float32)
        _ctx_2048c = jax.random.dirichlet(jax.random.fold_in(_rk, 512), 0.3 * jnp.ones((16,), jnp.float32), (4, 256))
        _ctx_2048t = jnp.einsum('bsk,bkd->bsd', _ctx_2048c, _ctx_2048P)
        _ctx_2048t = _ctx_2048t * jax.lax.rsqrt(jnp.mean(jnp.square(_ctx_2048t)) + 1e-12) * 0.953939
        ctx_2048 = 6.82029e-06 + 0.0200006 * (_ctx_2048t + 0.3 * jax.random.normal(jax.random.fold_in(_rk, 612), (4, 256, 256), jnp.float32))
        return (x, itok_BxS_13_99985, ctx_2048)
    x, itok_BxS_13_99985, ctx_2048 = _rec_inputs()

    def _L0_attn_setup():
        import jax, jax.numpy as jnp
        import numpy as np
        HIDDEN = 256
        HEADS = 16
        HEAD_DIM = HIDDEN // HEADS
        SCALE = 1.0 / np.sqrt(HEAD_DIM).astype(np.float32)
        key = jax.random.key(seed)
        k1, k2, k3, k4, k5 = jax.random.split(key, 5)
        B, QL = (8, 128)
        NB, BS = (32, 128)
        query = jax.random.normal(k1, (B, QL, HIDDEN), dtype=jnp.float32)
        kv_k = jax.random.normal(k2, (NB, BS, HIDDEN), dtype=jnp.float32)
        kv_v = jax.random.normal(k3, (NB, BS, HIDDEN), dtype=jnp.float32)
        Wq = jax.random.normal(k4, (HIDDEN, HIDDEN), dtype=jnp.float32) * (1.0 / np.sqrt(HIDDEN))
        Wo = jax.random.normal(k5, (HIDDEN, HIDDEN), dtype=jnp.float32) * (1.0 / np.sqrt(HIDDEN))
        return {'query': query, 'kv_k': kv_k, 'kv_v': kv_v, 'Wq': Wq, 'Wo': Wo}
    _L0_attn_all = _L0_attn_setup()
    _L0_attn_in = {k: v for k, v in _L0_attn_all.items() if k in ('kv_k', 'kv_v', 'Wq', 'Wo')}
    del _L0_attn_all

    def _L0_xattn_setup():
        import jax, jax.numpy as jnp
        import numpy as np
        B, S, D = (4, 512, 256)
        E = 4
        F = 1024 // E
        VOCAB = 12500
        key = jax.random.key(seed)
        k1, k2, k3, k4, k5 = jax.random.split(key, 5)
        hidden_states = jax.random.normal(k1, (B, S, D), dtype=jnp.float32)
        token_ids = jax.random.randint(k2, (B, S), 0, VOCAB, dtype=jnp.int64)
        Wg = jax.random.normal(k3, (E, F, D), dtype=jnp.float32) * 0.02
        Wu = jax.random.normal(k4, (E, F, D), dtype=jnp.float32) * 0.02
        Wd = jax.random.normal(k5, (E, D, F), dtype=jnp.float32) * 0.02
        return {'hidden_states': hidden_states, 'token_ids': token_ids, 'Wg': Wg, 'Wu': Wu, 'Wd': Wd}
    _L0_xattn_all = _L0_xattn_setup()
    _L0_xattn_in = {k: v for k, v in _L0_xattn_all.items() if k in ()}
    del _L0_xattn_all

    def _L0_ffn_setup():
        import jax, jax.numpy as jnp
        import numpy as np
        HIDDEN = 256
        FFN = 176
        N_EXPERTS = 64
        TOP_K = 6
        N_SHARED = 2
        SHARED_FFN = FFN * N_SHARED
        ROUTED_SCALING = 1.0
        EPS = 1e-20

        def _moe_forward(x, gate_w, w_gate_up, w_down, ws_gate_up, ws_down):
            T = x.shape[0]
            logits = jnp.einsum('th,eh->te', x.astype(jnp.float32), gate_w.astype(jnp.float32))
            scores = jax.nn.softmax(logits, axis=-1)
            topk_w, topk_ids = jax.lax.top_k(scores, TOP_K)
            topk_w = topk_w / (jnp.sum(topk_w, axis=-1, keepdims=True) + EPS)
            topk_w = topk_w * ROUTED_SCALING
            comb = jnp.zeros((T, N_EXPERTS), dtype=x.dtype)
            comb = comb.at[jnp.arange(T)[:, None], topk_ids].add(topk_w.astype(x.dtype))
            gu = jnp.einsum('th,efh->tef', x, w_gate_up)
            g, u = (gu[..., :FFN], gu[..., FFN:])
            act = jax.nn.silu(g) * u
            act = act * comb[:, :, None]
            routed = jnp.einsum('tef,ehf->th', act, w_down)
            sgu = jnp.einsum('th,fh->tf', x, ws_gate_up)
            sg, su = (sgu[..., :SHARED_FFN], sgu[..., SHARED_FFN:])
            shared = jnp.einsum('tf,hf->th', jax.nn.silu(sg) * su, ws_down)
            return routed + shared
        key = jax.random.key(seed)
        k0, k1, k2, k3, k4, k5 = jax.random.split(key, 6)
        hidden_states = jax.random.normal(k0, (1, 32, HIDDEN), dtype=jnp.float32)
        gate_w = jax.random.normal(k1, (N_EXPERTS, HIDDEN), dtype=jnp.float32) * 0.05
        w_gate_up = jax.random.normal(k2, (N_EXPERTS, 2 * FFN, HIDDEN), dtype=jnp.float32) * 0.02
        w_down = jax.random.normal(k3, (N_EXPERTS, HIDDEN, FFN), dtype=jnp.float32) * 0.02
        ws_gate_up = jax.random.normal(k4, (2 * SHARED_FFN, HIDDEN), dtype=jnp.float32) * 0.02
        ws_down = jax.random.normal(k5, (HIDDEN, SHARED_FFN), dtype=jnp.float32) * 0.02
        return {'hidden_states': hidden_states, 'gate_w': gate_w, 'w_gate_up': w_gate_up, 'w_down': w_down, 'ws_gate_up': ws_gate_up, 'ws_down': ws_down}
    _L0_ffn_all = _L0_ffn_setup()
    _L0_ffn_in = {k: v for k, v in _L0_ffn_all.items() if k in ('gate_w', 'w_gate_up', 'w_down', 'ws_gate_up', 'ws_down')}
    del _L0_ffn_all
    return {'x': x, 'itok_BxS_13_99985': itok_BxS_13_99985, 'ctx_2048': ctx_2048, 'L0_attn_kv_k': _L0_attn_in['kv_k'], 'L0_attn_kv_v': _L0_attn_in['kv_v'], 'L0_attn_Wq': _L0_attn_in['Wq'], 'L0_attn_Wo': _L0_attn_in['Wo'], 'L0_ffn_gate_w': _L0_ffn_in['gate_w'], 'L0_ffn_w_gate_up': _L0_ffn_in['w_gate_up'], 'L0_ffn_w_down': _L0_ffn_in['w_down'], 'L0_ffn_ws_gate_up': _L0_ffn_in['ws_gate_up'], 'L0_ffn_ws_down': _L0_ffn_in['ws_down']}

def reference(x, itok_BxS_13_99985, ctx_2048, L0_attn_kv_k, L0_attn_kv_v, L0_attn_Wq, L0_attn_Wo, L0_ffn_gate_w, L0_ffn_w_gate_up, L0_ffn_w_down, L0_ffn_ws_gate_up, L0_ffn_ws_down):
    import jax
    import jax.numpy as jnp

    def _L0_attn_ref(query, kv_k, kv_v, Wq, Wo):
        import jax, jax.numpy as jnp
        import numpy as np
        HIDDEN = 256
        HEADS = 16
        HEAD_DIM = HIDDEN // HEADS
        SCALE = 1.0 / np.sqrt(HEAD_DIM).astype(np.float32)
        B, QL, _ = query.shape
        NB, BS, _ = kv_k.shape
        KV = NB * BS
        Q = (query @ Wq.T).reshape(B, QL, HEADS, HEAD_DIM)
        K = kv_k.reshape(KV, HEADS, HEAD_DIM)
        V = kv_v.reshape(KV, HEADS, HEAD_DIM)
        scores = jnp.einsum('bqhd,khd->bhqk', Q, K) * SCALE
        attn = jax.nn.softmax(scores, axis=-1)
        out = jnp.einsum('bhqk,khd->bqhd', attn, V).reshape(B, QL, HIDDEN)
        return out @ Wo.T

    def _L0_xattn_ref(hidden_states, token_ids, Wg, Wu, Wd):
        import jax, jax.numpy as jnp
        import numpy as np
        B, S, D = (4, 512, 256)
        E = 4
        F = 1024 // E
        VOCAB = 12500
        tokens_per_expert = VOCAB // E
        tid = jnp.clip(token_ids, 0, VOCAB - 1)
        expert_ids = jnp.minimum(tid // tokens_per_expert, E - 1)
        out = jnp.zeros_like(hidden_states)
        for e in range(E):
            g = jax.nn.silu(jnp.einsum('bsd,fd->bsf', hidden_states, Wg[e]))
            u = jnp.einsum('bsd,fd->bsf', hidden_states, Wu[e])
            y = jnp.einsum('bsf,df->bsd', g * u, Wd[e])
            out = jnp.where((expert_ids == e)[..., None], y, out)
        return out

    def _L0_ffn_ref(hidden_states, gate_w, w_gate_up, w_down, ws_gate_up, ws_down):
        import jax, jax.numpy as jnp
        import numpy as np
        HIDDEN = 256
        FFN = 176
        N_EXPERTS = 64
        TOP_K = 6
        N_SHARED = 2
        SHARED_FFN = FFN * N_SHARED
        ROUTED_SCALING = 1.0
        EPS = 1e-20

        def _moe_forward(x, gate_w, w_gate_up, w_down, ws_gate_up, ws_down):
            T = x.shape[0]
            logits = jnp.einsum('th,eh->te', x.astype(jnp.float32), gate_w.astype(jnp.float32))
            scores = jax.nn.softmax(logits, axis=-1)
            topk_w, topk_ids = jax.lax.top_k(scores, TOP_K)
            topk_w = topk_w / (jnp.sum(topk_w, axis=-1, keepdims=True) + EPS)
            topk_w = topk_w * ROUTED_SCALING
            comb = jnp.zeros((T, N_EXPERTS), dtype=x.dtype)
            comb = comb.at[jnp.arange(T)[:, None], topk_ids].add(topk_w.astype(x.dtype))
            gu = jnp.einsum('th,efh->tef', x, w_gate_up)
            g, u = (gu[..., :FFN], gu[..., FFN:])
            act = jax.nn.silu(g) * u
            act = act * comb[:, :, None]
            routed = jnp.einsum('tef,ehf->th', act, w_down)
            sgu = jnp.einsum('th,fh->tf', x, ws_gate_up)
            sg, su = (sgu[..., :SHARED_FFN], sgu[..., SHARED_FFN:])
            shared = jnp.einsum('tf,hf->th', jax.nn.silu(sg) * su, ws_down)
            return routed + shared
        B, S, H = hidden_states.shape
        x = hidden_states.reshape(-1, H)
        out = _moe_forward(x, gate_w, w_gate_up, w_down, ws_gate_up, ws_down)
        return out.reshape(B, S, H)
    x = _layernorm(x + _L0_attn_ref(x, L0_attn_kv_k, L0_attn_kv_v, L0_attn_Wq, L0_attn_Wo), axis=-1)
    x = _layernorm(x + _L0_xattn_ref(x, itok_BxS_13_99985, ctx_2048, ctx_2048, ctx_2048), axis=-1)
    x = _layernorm(x + _L0_ffn_ref(x, L0_ffn_gate_w, L0_ffn_w_gate_up, L0_ffn_w_down, L0_ffn_ws_gate_up, L0_ffn_ws_down), axis=-1)
    return x

_drawn_inputs = setup_inputs


def setup_inputs(seed=0):
    import zlib

    import numpy as np

    out = dict(_drawn_inputs(seed))
    spreads = {}
    factors = {'L0_ffn_gate_w': 8.0,
     'L0_ffn_w_gate_up': 8.0,
     'L0_ffn_w_down': 8.0,
     'L0_ffn_ws_gate_up': 2.846,
     'L0_ffn_ws_down': 2.839}
    for name, (base, spread) in spreads.items():
        noise = np.random.default_rng([zlib.crc32(name.encode()), seed]).standard_normal(out[name].shape)
        drawn = base * np.exp(spread * noise) if base else spread * noise
        out[name] = jnp.asarray(drawn.astype(out[name].dtype))
    for name, factor in factors.items():
        out[name] = (out[name] * factor).astype(out[name].dtype)
    return out
```

```python
import numpy as np
import concourse.bass as bass
from concourse import mybir
from contextlib import ExitStack

F32 = mybir.dt.float32
BF16 = mybir.dt.bfloat16
I32 = mybir.dt.int32
U32 = mybir.dt.uint32
ALU = mybir.AluOpType
ACT = mybir.ActivationFunctionType
AX = mybir.AxisListType

P = 128
T, D = 1024, 256
DC = D // P
QT = T // P
HEADS, HD = 16, 16
KV = 4096
KT = KV // P
SCALE = 1.0 / 4.0
EPS = 1e-5

GROUPS = [(0, 0), (0, 1), (1, 0), (1, 1), (2, 0), (0, 2)]
ROWS = len(GROUPS) * HD
MROWS = 3
RING = 4
AHEAD = 3
HALF = 512
PAIRS = QT * KV // 1024
FIRST_PAIRS = 4
STEPS = 2 * KT
SG = KT // 4
CH = 1024

E1 = 4
F1 = 256
VOCAB = 12500


def attention(nc, ctx, a, oT):
    sb = lambda name, shape, dt: ctx.enter_context(nc.sbuf_tensor(name, shape, dt))
    pb = lambda name, shape: ctx.enter_context(nc.psum_tensor(name, shape, F32))
    sem = lambda name: ctx.enter_context(nc.semaphore(name))

    flat = oT[:, :, :].rearrange("p h t -> p (h t)")
    taken = [0]

    def early(*shape):
        size = int(np.prod(shape))
        view = flat[:, taken[0]:taken[0] + size]
        taken[0] += size
        if len(shape) > 1:
            view = view.rearrange("p (a n) -> p a n", a=shape[0])
        return view

    def early_bf16(*shape):
        size = int(np.prod(shape))
        view = flat[:, taken[0]:taken[0] + size // 2].bitcast(BF16)
        taken[0] += size // 2
        names = {2: ("p (a n) -> p a n", {"a": shape[0]}),
                 3: ("p (a b n) -> p a b n", {"a": shape[0], "b": shape[1] if len(shape) > 2 else 1})}
        return view.rearrange(names[len(shape)][0], **names[len(shape)][1])

    xT = early(DC, T)
    wqT = early(DC, D)
    kstack = [sb(f"kstack{b}", [ROWS + MROWS, KV], BF16) for b in range(RING)]
    qstack = [sb(f"qstack{b}", [ROWS + MROWS, T], BF16) for b in range(RING)]
    ksrc = [[early(CH) for i in range(2)], [sb(f"ksrc{i}", [P, CH], F32) for i in range(2)]]
    kres = [[early(CH) for i in range(2)], [sb(f"kres{i}", [P, CH], F32) for i in range(2)]]
    kpart = [[early_bf16(3, CH) for i in range(2)], [sb(f"kpart{i}", [P, 3, CH], BF16) for i in range(2)]]
    qpart = early_bf16(4, 3, HALF)
    qres = kres[0][0]
    vstage = [sb(f"vstage{b}", [P, KT, HD], F32) for b in range(2)]
    vpad = [sb(f"vpad{b}", [P, KT, 32], F32) for b in range(2)]
    ones = sb("ones", [P, KT, HD], F32)
    weights = sb("weights", [P, 2, 4, T], F32)
    mx4 = sb("mx4", [P, QT, 4], F32)
    mneg = sb("mneg", [P, QT], F32)
    mres = sb("mres", [P, QT], F32)
    mres2 = sb("mres2", [P, QT], F32)
    m3 = sb("m3", [P, QT, 3], BF16)
    ident = sb("ident_bf", [P, P], BF16)

    Mb = pb("Mb", [P, 2, 1024])
    Sb = pb("Sb", [P, 2, HALF])
    Ob = pb("Ob", [P, 2, HALF])
    Qb = Mb[:, :, :].rearrange("p a (b n) -> p (a b) n", b=2)

    kparts = nc.dram_tensor("kparts", [3, D, KV], BF16, kind="Internal").ap()
    qparts = nc.dram_tensor("qparts", [3, D, T], BF16, kind="Internal").ap()

    s_x = sem("s_x")
    s_ksrc = [sem(f"s_ksrc{c}{i}") for c in range(DC) for i in range(2)]
    s_q = sem("s_q")
    s_qc = sem("s_qc")
    s_qs = sem("s_qs")
    s_kc = sem("s_kc")
    s_ks = sem("s_ks")
    s_kp = sem("s_kp")
    s_kpo = sem("s_kpo")
    s_qw = sem("s_qw")
    s_kw = [[sem(f"s_kw{c}{i}") for i in range(2)] for c in range(DC)]
    s_const = sem("s_const")
    s_stack = [sem(f"s_stack{b}") for b in range(RING)]
    s_vload = [sem(f"s_vload{b}") for b in range(2)]
    s_v = sem("s_v")
    s_mx = sem("s_mx")
    s_mred = sem("s_mred")
    s_mch = sem("s_mch")
    s_m3 = sem("s_m3")
    s_mt = sem("s_mt")
    s_qm = sem("s_qm")
    s_st = sem("s_st")
    s_exp = sem("s_exp")
    s_pv = sem("s_pv")
    s_ot = sem("s_ot")

    block = ctx.enter_context(nc.Block())
    NCH = KV // CH
    LOADED = 2 * len(GROUPS) * 16

    @block.sync
    def _(sp):
        def load_chunk(c, i):
            if i >= 2:
                if c == 0:
                    sp.wait_ge(s_ks, 2 * (i - 1))
                else:
                    sp.wait_ge(s_kp, i - 1)
            sp.dma_start(ksrc[c][i % 2][:, :], a["kT"][:, c, i * CH:(i + 1) * CH]).then_inc(s_ksrc[2 * c + i % 2], 16)

        def store_chunk(c, i):
            if c == 0:
                sp.wait_ge(s_ks, 2 * (i + 1))
            else:
                sp.wait_ge(s_kp, i + 1)
            for part in range(3):
                sp.dma_start(kparts[part, c * P:(c + 1) * P, i * CH:(i + 1) * CH],
                             kpart[c][i % 2][:, part, :]).then_inc(s_kw[c][i % 2], 16)

        def load_stack(h, b):
            for g, (kp, qp) in enumerate(GROUPS):
                rows = slice(g * HD, (g + 1) * HD)
                sp.dma_start(kstack[b][rows, :], kparts[kp, bass.ds(h * HD, HD), :]).then_inc(s_stack[b], 16)
                sp.dma_start(qstack[b][rows, :], qparts[qp, bass.ds(h * HD, HD), :]).then_inc(s_stack[b], 16)

        def load_v(h, b):
            sp.dma_start(vstage[b][:, :, :], a["v"][bass.ds(h, 1), :, :].rearrange("o p n -> p (o n)")
                         .rearrange("p (k d) -> p k d", k=KT)).then_inc(s_vload[b], 16)

        sp.dma_start(wqT[:, :, :], a["wqT"]).then_inc(s_x, 16)
        sp.dma_start(xT[:, :, :], a["xT"]).then_inc(s_x, 16)
        for i in range(2):
            load_chunk(0, i)
        for i in range(NCH):
            if i + 2 < NCH:
                load_chunk(0, i + 2)
            store_chunk(0, i)
        load_v(0, 0)
        for n in range(4):
            sp.wait_ge(s_qs, 2 * (n + 1))
            c, half = n // 2, n % 2
            for part in range(3):
                sp.dma_start(qparts[part, c * P:(c + 1) * P, half * HALF:(half + 1) * HALF],
                             qpart[:, n, part, :]).then_inc(s_qw, 16)
        sp.wait_ge(s_qw, 12 * 16)
        for i in range(2):
            sp.wait_ge(s_kw[0][i], 3 * 16 * (NCH // 2))
        for h in range(AHEAD):
            load_stack(h, h)
        for i in range(2):
            load_chunk(1, i)
        for i in range(NCH):
            if i + 2 < NCH:
                load_chunk(1, i + 2)
            store_chunk(1, i)
        for i in range(2):
            sp.wait_ge(s_kw[1][i], 3 * 16 * (NCH // 2))

        def head(h, b, stack, v):
            if v:
                sp.wait_ge(s_v, h)
                load_v(h + 1, (b + 1) % 2)
            if stack:
                sp.wait_ge(s_st, h * STEPS)
                sp.wait_ge(s_qm, h)
                load_stack(h + AHEAD, (b + AHEAD) % RING)

        load_v(1, 1)
        load_stack(AHEAD, AHEAD)
        for h in range(1, RING):
            head(h, h, True, True)
        with sp.Fori(1, HEADS // RING - 1) as i:
            for b in range(RING):
                head(RING * i + b, b, True, True)
        for h in range(HEADS - RING, HEADS):
            head(h, h % RING, h + AHEAD < HEADS, h + 1 < HEADS)

    @block.gpsimd
    def _(pool):
        order = [0]

        def link(ins):
            order[0] += 1
            ins.then_inc(s_kpo, 1)
            pool.wait_ge(s_kpo, order[0])

        link(nc.gpsimd.memset(ident[:, :], 0.0))
        link(nc.gpsimd.affine_select(out=ident[:, :], in_=ident[:, :], compare_op=ALU.not_equal, fill=1.0, base=0,
                                     pattern=[[-1, P]], channel_multiplier=1))
        pool.sem_inc(s_const, 1)
        link(nc.gpsimd.memset(ones[:, :, :], 1.0))
        for b in range(2):
            link(nc.gpsimd.memset(vpad[b][:, :, HD:32], 0.0))
            link(nc.gpsimd.memset(vpad[b][:, :, HD:HD + 1], 1.0))

        def pad_v(h, b, nth, waits):
            pool.wait_ge(s_vload[b], 16 * nth)
            if waits:
                pool.wait_ge(s_pv, 4 + (h - 1) * 2 * SG)
                pool.wait_ge(s_v, h)
            nc.gpsimd.tensor_tensor(vpad[b][:, :, 0:HD], vstage[b][:, :, :], ones[:, :, :],
                                    ALU.mult).then_inc(s_v, 1)

        pad_v(0, 0, 1, False)
        pool.wait_ge(s_v, 1)
        for i in range(NCH):
            pool.wait_ge(s_ksrc[2 + i % 2], 16 * (i // 2 + 1))
            if i >= 2:
                pool.wait_ge(s_kw[1][i % 2], 48 * (i // 2))
            src, res, part = ksrc[1][i % 2], kres[1][i % 2], kpart[1][i % 2]
            link(nc.gpsimd.tensor_copy(part[:, 0, :], src[:, :]))
            link(nc.gpsimd.tensor_tensor(res[:, :], src[:, :], part[:, 0, :], ALU.subtract))
            link(nc.gpsimd.tensor_copy(part[:, 1, :], res[:, :]))
            nc.gpsimd.tensor_tensor(part[:, 2, :], res[:, :], part[:, 1, :], ALU.subtract).then_inc(s_kp, 1)
            pool.wait_ge(s_kp, i + 1)
        pad_v(1, 1, 1, False)
        for h in range(2, RING):
            pad_v(h, h % 2, h // 2 + 1, True)
        with pool.Fori(1, HEADS // RING) as i:
            for b in range(RING):
                pad_v(RING * i + b, b % 2, 2 * i + b // 2 + 1, True)

    @block.scalar
    def _(act):
        for n in range(4):
            act.wait_ge(s_q, n + 1)
            nc.scalar.activation(qpart[:, n, 0, :], Qb[:, n, :], ACT.Copy).then_inc(s_qc, 1)
            act.wait_ge(s_qs, 2 * n + 1)
            nc.scalar.activation(qpart[:, n, 1, :], qres[:, (n % 2) * HALF:(n % 2 + 1) * HALF],
                                 ACT.Copy).then_inc(s_qc, 1)
        for i in range(NCH):
            act.wait_ge(s_ksrc[i % 2], 16 * (i // 2 + 1))
            if i >= 2:
                act.wait_ge(s_kw[0][i % 2], 48 * (i // 2))
            nc.scalar.activation(kpart[0][i % 2][:, 0, :], ksrc[0][i % 2][:, :], ACT.Copy).then_inc(s_kc, 1)
            act.wait_ge(s_ks, 2 * i + 1)
            nc.scalar.activation(kpart[0][i % 2][:, 1, :], kres[0][i % 2][:, :], ACT.Copy).then_inc(s_kc, 1)

        def move_rows(h, b):
            act.wait_ge(s_mt, h + 1)
            nc.scalar.activation(qstack[b][ROWS:ROWS + MROWS, :], Sb[ROWS:ROWS + MROWS, :, :]
                                 .rearrange("p a n -> p (a n)"), ACT.Copy).then_inc(s_qm, 1)

        def head(h, b, last):
            for n in range(STEPS):
                kt, half = n // 2, n % 2
                s = kt // 4
                act.wait_ge(s_st, STEPS * h + n + 1)
                if n % 8 < 2:
                    act.wait_ge(s_pv, 2 * SG * h + 2 * s + half + 1)
                nc.scalar.activation(weights[:, s % 2, kt % 4, half * HALF:(half + 1) * HALF], Sb[:, n % 2, :],
                                     ACT.Exp, scale=SCALE).then_inc(s_exp, 1)
            if not last:
                move_rows(h + 1, (b + 1) % RING)
            act.wait_ge(s_pv, 4 + 2 * SG * (h + 1))
            nc.scalar.activation(oT[:, bass.ds(h, 1), :].rearrange("p o n -> p (o n)"),
                                 Ob[:, :, :].rearrange("p a n -> p (a n)"), ACT.Copy).then_inc(s_ot, 1)

        move_rows(0, 0)
        with act.Fori(0, HEADS // RING - 1) as i:
            for b in range(RING):
                head(RING * i + b, b, False)
        for h in range(HEADS - RING, HEADS):
            head(h, h % RING, h == HEADS - 1)

    @block.vector
    def _(dve):
        for b in range(RING):
            nc.vector.memset(kstack[b][ROWS:ROWS + MROWS, :], 1.0).then_inc(s_const, 1)
        for n in range(4):
            res = qres[:, (n % 2) * HALF:(n % 2 + 1) * HALF]
            dve.wait_ge(s_qc, 2 * n + 1)
            nc.vector.tensor_tensor(res, Qb[:, n, :], qpart[:, n, 0, :], ALU.subtract).then_inc(s_qs, 1)
            dve.wait_ge(s_qc, 2 * n + 2)
            dve.wait_ge(s_qs, 2 * n + 1)
            nc.vector.tensor_tensor(qpart[:, n, 2, :], res, qpart[:, n, 1, :], ALU.subtract).then_inc(s_qs, 1)
        dve.wait_ge(s_qs, 8)
        for i in range(NCH):
            src, res, part = ksrc[0][i % 2], kres[0][i % 2], kpart[0][i % 2]
            dve.wait_ge(s_kc, 2 * i + 1)
            nc.vector.tensor_tensor(res[:, :], src[:, :], part[:, 0, :], ALU.subtract).then_inc(s_ks, 1)
            dve.wait_ge(s_kc, 2 * i + 2)
            dve.wait_ge(s_ks, 2 * i + 1)
            nc.vector.tensor_tensor(part[:, 2, :], res[:, :], part[:, 1, :], ALU.subtract).then_inc(s_ks, 1)

        def link(ins, count):
            ins.then_inc(s_mch, 1)
            dve.wait_ge(s_mch, count)

        CHAIN = 5

        def maxima(h, first):
            for j in range(PAIRS):
                dve.wait_ge(s_mx, PAIRS * h + j + 1)
                nc.vector.tensor_reduce(mx4[:, j // 4, j % 4:j % 4 + 1], Mb[:, j % 2, :], AX.X,
                                        ALU.max).then_inc(s_mred, 1)
            dve.wait_ge(s_mred, PAIRS * (h + 1))
            if not first:
                dve.wait_ge(s_mt, h)
            n = CHAIN * h
            link(nc.vector.tensor_reduce(mres[:, :], mx4[:, :, :], AX.X, ALU.max), n + 1)
            link(nc.vector.tensor_scalar(mneg[:, :], mres[:, :], -1.0, None, ALU.mult), n + 2)
            link(nc.vector.tensor_copy(m3[:, :, 0], mneg[:, :]), n + 3)
            link(nc.vector.tensor_tensor(mres2[:, :], mneg[:, :], m3[:, :, 0], ALU.subtract), n + 4)
            link(nc.vector.tensor_copy(m3[:, :, 1], mres2[:, :]), n + 5)
            nc.vector.tensor_tensor(m3[:, :, 2], mres2[:, :], m3[:, :, 1], ALU.subtract).then_inc(s_m3, 1)

        maxima(0, True)
        with dve.Fori(0, HEADS // RING - 1) as i:
            for b in range(RING):
                maxima(RING * i + b + 1, False)
        for h in range(HEADS - RING + 1, HEADS):
            maxima(h, False)

    @block.tensor
    def _(pe):
        pe.wait_ge(s_x, 32)
        for n in range(4):
            c, half = n // 2, n % 2
            for k in range(DC):
                last = nc.tensor.matmul(Qb[:, n, :], wqT[:, k, c * P:(c + 1) * P],
                                        xT[:, k, half * HALF:(half + 1) * HALF], start=(k == 0), stop=(k == DC - 1))
            last.then_inc(s_q, 1)

        def pair(h, b, j, prologue):
            if not (prologue and j < 2):
                pe.wait_ge(s_mred, PAIRS * h + j - 1)
            qt, kc = j // 4, j % 4
            for u in range(2):
                k0 = kc * 1024 + u * HALF
                last = nc.tensor.matmul(Mb[:, j % 2, u * HALF:(u + 1) * HALF], qstack[b][0:ROWS, qt * P:(qt + 1) * P],
                                        kstack[b][0:ROWS, k0:k0 + HALF], start=True, stop=True)
            last.then_inc(s_mx, 1)

        def max_rows(h):
            pe.wait_ge(s_m3, h + 1)
            for qt in range(QT):
                last = nc.tensor.matmul(Sb[ROWS:ROWS + MROWS, qt // 4, (qt % 4) * P:(qt % 4 + 1) * P], m3[:, qt, :],
                                        ident[:, :], start=True, stop=True)
            last.then_inc(s_mt, 1)

        def weigh(h, b, s, half):
            if s == 0 and half == 0:
                pe.wait_ge(s_v, h + 1)
                pe.wait_ge(s_ot, h + 1)
            pe.wait_ge(s_exp, STEPS * h + 8 * s + 7 + half)
            for g in range(4):
                last = nc.tensor.matmul(Ob[32 * g:32 * g + 32, half, :], vpad[b % 2][:, 4 * s + g, :],
                                        weights[:, s % 2, g, half * HALF:(half + 1) * HALF],
                                        start=(s == 0), stop=(s == SG - 1))
            last.then_inc(s_pv, 1)

        def head(h, b, last):
            nb = (b + 1) % RING
            for j in range(0 if last else FIRST_PAIRS):
                pair(h + 1, nb, j, False)
            pe.wait_ge(s_qm, h + 1)
            for n in range(STEPS):
                kt, half = n // 2, n % 2
                if n >= 2:
                    pe.wait_ge(s_exp, STEPS * h + n - 1)
                nc.tensor.matmul(Sb[:, n % 2, :], kstack[b][:, kt * P:(kt + 1) * P],
                                 qstack[b][:, half * HALF:(half + 1) * HALF], start=True, stop=True).then_inc(s_st, 1)
                if half == 1 and not last and kt + FIRST_PAIRS < PAIRS:
                    pair(h + 1, nb, kt + FIRST_PAIRS, False)
                if n % 4 == 3 and kt >= 4:
                    weigh(h, b, kt // 4 - 1, kt % 4 // 2)
            if not last:
                pe.wait_ge(s_exp, STEPS * (h + 1))
                max_rows(h + 1)
            for half in range(2):
                weigh(h, b, SG - 1, half)

        pe.wait_ge(s_qs, 8)
        pe.wait_ge(s_const, 1 + RING)
        pe.wait_ge(s_stack[0], LOADED)
        for j in range(PAIRS):
            pair(0, 0, j, True)
        max_rows(0)
        pe.sem_inc(s_pv, 4)
        pe.sem_inc(s_ot, 1)

        with pe.Fori(0, HEADS // RING - 1) as i:
            for b in range(RING):
                pe.wait_ge(s_stack[(b + 1) % RING], LOADED * (i + 1 + (b + 1) // RING))
                head(RING * i + b, b, False)
        for h in range(HEADS - RING, HEADS):
            if h + 1 < HEADS:
                pe.wait_ge(s_stack[(h + 1) % RING], LOADED * ((h + 1) // RING + 1))
            head(h, h % RING, h == HEADS - 1)


def project_and_experts(nc, ctx, a, oT, x2):
    sb = lambda name, shape, dt: ctx.enter_context(nc.sbuf_tensor(name, shape, dt))
    sem = lambda name: ctx.enter_context(nc.semaphore(name))
    banks = [ctx.enter_context(nc.psum_tensor(f"bank{i}", [P, 2, HALF], F32)) for i in range(4)]

    x = sb("x", [P, QT, D], F32)
    woT = sb("woT", [P, 4, D], F32)
    ctxT = sb("ctxT", [P, E1, DC, F1], F32)
    ids = sb("ids", [P, T], I32)
    idf = sb("idf", [P, T], F32)
    ge = sb("ge", [P, 3, T], F32)
    mask = sb("mask", [P, E1, T], F32)
    ident = sb("ident", [P, P], F32)
    pick = sb("pick", [P, 2, 32], F32)
    att = sb("att", [P, 4, T], F32)
    rden = sb("rden", [P, T], F32)
    stats = sb("stats", [P, QT, 6], F32)
    mv = sb("mv", [P, QT, 2], F32)
    var = sb("var", [P, QT], F32)
    std = sb("std", [P, QT], F32)
    rstd = sb("rstd", [P, QT], F32)
    x1 = sb("x1", [P, QT, D], F32)
    x1T = sb("x1T", [P, DC, T], F32)
    xm = sb("xm", [P, 2, DC, T], F32)
    silu = sb("silu", [P, 2, HALF], F32)
    hid = oT[:, 0:E1 * 2, :].rearrange("p (e f) t -> p e f t", f=2)

    s_ld = [sem(f"s_ld{i}") for i in range(4)]
    s_c = sem("s_c")
    s_po = sem("s_po")
    s_mask = sem("s_mask")
    s_u = sem("s_u")
    s_dch = sem("s_dch")
    s_att = sem("s_att")
    s_proj = sem("s_proj")
    s_x1 = sem("s_x1")
    s_tr = sem("s_tr")
    s_x1T = sem("s_x1T")
    s_xm = sem("s_xm")
    s_z = sem("s_z")
    s_si = sem("s_si")
    s_h = sem("s_h")
    s_y = sem("s_y")
    s_x2 = sem("s_x2")
    s_sum = sem("s_sum")
    s_var = sem("s_var")
    s_std = sem("s_std")

    block = ctx.enter_context(nc.Block())

    @block.sync
    def _(sp):
        sp.dma_start(woT[:, :, :], a["woT"]).then_inc(s_ld[0], 16)
        sp.dma_start(x[:, :, :], a["x"]).then_inc(s_ld[0], 16)
        sp.dma_start(ids[:, :], a["ids"].rearrange("(o t) -> o t", o=1).partition_broadcast(P)
                     if False else a["ids"].rearrange("(o t) -> o t", o=1).broadcast_to([P, T])).then_inc(s_ld[1], 16)
        sp.dma_start(ctxT[:, :, :, :], a["ctxT"]).then_inc(s_ld[2], 16)

    @block.gpsimd
    def _(pool):
        order = [0]

        def link(ins):
            order[0] += 1
            ins.then_inc(s_po, 1)
            pool.wait_ge(s_po, order[0])

        link(nc.gpsimd.memset(pick[:, :, :], 0.0))
        for g in range(4):
            link(nc.gpsimd.affine_select(out=pick[:, 0, :], in_=pick[:, 0, :], compare_op=ALU.not_equal, fill=1.0,
                                         base=-32 * g, pattern=[[-1, 32]], channel_multiplier=1))
            link(nc.gpsimd.affine_select(out=pick[:, 1, :], in_=pick[:, 1, :], compare_op=ALU.not_equal, fill=1.0,
                                         base=-32 * g - HD, pattern=[[0, 32]], channel_multiplier=1))
        link(nc.gpsimd.memset(ident[:, :], 0.0))
        link(nc.gpsimd.affine_select(out=ident[:, :], in_=ident[:, :], compare_op=ALU.not_equal, fill=1.0, base=0,
                                     pattern=[[-1, P]], channel_multiplier=1))
        pool.sem_inc(s_c, 1)
        pool.wait_ge(s_ld[1], 16)
        link(nc.gpsimd.tensor_copy(idf[:, :], ids[:, :]))
        for e in range(3):
            link(nc.gpsimd.tensor_scalar(ge[:, e, :], idf[:, :], float((e + 1) * (VOCAB // E1)), None, ALU.is_ge))
        link(nc.gpsimd.tensor_scalar(mask[:, 0, :], ge[:, 0, :], -1.0, 1.0, ALU.mult, ALU.add))
        for e in range(1, 3):
            link(nc.gpsimd.tensor_tensor(mask[:, e, :], ge[:, e - 1, :], ge[:, e, :], ALU.subtract))
        link(nc.gpsimd.tensor_copy(mask[:, 3, :], ge[:, 2, :]))
        pool.wait_ge(s_x1T, QT)
        for e in range(E1):
            if e >= 2:
                pool.wait_ge(s_z, 4 * (e - 1))
            for c in range(DC):
                nc.gpsimd.tensor_tensor(xm[:, e % 2, c, :], x1T[:, c, :], mask[:, e, :], ALU.mult).then_inc(s_xm, 1)
                pool.wait_ge(s_xm, DC * e + c + 1)

    @block.scalar
    def _(act):
        def root(nth):
            act.wait_ge(s_var, nth)
            nc.scalar.activation(std[:, :], var[:, :], ACT.Sqrt).then_inc(s_std, 1)

        root(1)
        for qt in range(QT):
            act.wait_ge(s_tr, qt + 1)
            nc.scalar.activation(x1T[:, :, qt * P:(qt + 1) * P], banks[2 + qt % 2][:, 0, 0:D]
                                 .rearrange("p (c n) -> p c n", c=DC), ACT.Copy).then_inc(s_x1T, 1)
        for n in range(4 * E1):
            act.wait_ge(s_z, n + 1)
            if n >= 2:
                act.wait_ge(s_h, n - 1)
            nc.scalar.activation(silu[:, n % 2, :], banks[n % 4][:, 0, :], ACT.Silu).then_inc(s_si, 1)
        root(2)

    @block.vector
    def _(dve):
        order = [0]

        def link(ins):
            order[0] += 1
            ins.then_inc(s_dch, 1)
            dve.wait_ge(s_dch, order[0])

        for g in range(4):
            dve.wait_ge(s_u, g + 1)
            sums, dens = banks[g % 2 * 2], banks[g % 2 * 2 + 1]
            link(nc.vector.reciprocal(rden[:, :], dens[:, :, :].rearrange("p a n -> p (a n)")))
            nc.vector.tensor_tensor(att[:, g, :], sums[:, :, :].rearrange("p a n -> p (a n)"), rden[:, :],
                                    ALU.mult).then_inc(s_att, 1)
            dve.wait_ge(s_att, g + 1)

        def statistics(qt, bank, base):
            nc.vector.tensor_tensor(base, bank, base, ALU.add).then_inc(s_sum, 1)
            sums[0] += 1
            dve.wait_ge(s_sum, sums[0])
            link(nc.vector.bn_stats(stats[:, qt, :], base))
            link(nc.vector.bn_aggr(mv[:, qt, :], stats[:, qt, :]))

        def deviations(nth):
            nc.vector.tensor_scalar(var[:, :], mv[:, :, 1], EPS, None, ALU.add).then_inc(s_var, 1)
            dve.wait_ge(s_std, nth)
            link(nc.vector.reciprocal(rstd[:, :], std[:, :]))

        def normalise(qt, out, base, done):
            nc.vector.tensor_scalar(out, base, mv[:, qt, 0:1], rstd[:, qt:qt + 1], ALU.subtract,
                                    ALU.mult).then_inc(done, 1)

        sums = [0]
        dve.wait_ge(s_ld[0], 32)
        for qt in range(QT):
            dve.wait_ge(s_proj, qt + 1)
            statistics(qt, banks[qt % 2][:, 0, 0:D], x[:, qt, :])
        deviations(1)
        for qt in range(QT):
            normalise(qt, x1[:, qt, :], x[:, qt, :], s_x1)
        for n in range(4 * E1):
            e, f, half = n // 4, n // 2 % 2, n % 2
            dve.wait_ge(s_si, n + 1)
            nc.vector.tensor_tensor(hid[:, e, f, half * HALF:(half + 1) * HALF], banks[n % 4][:, 0, :],
                                    silu[:, n % 2, :], ALU.mult).then_inc(s_h, 1)
        dve.wait_ge(s_x1, QT)
        for qt in range(QT):
            dve.wait_ge(s_y, qt + 1)
            statistics(qt, banks[qt % 2][:, 0, 0:D], x1[:, qt, :])
        deviations(2)
        for qt in range(QT):
            normalise(qt, x2[:, qt, :], x1[:, qt, :], s_x2)

    @block.tensor
    def _(pe):
        pe.wait_ge(s_c, 1)
        for g in range(4):
            if g >= 2:
                pe.wait_ge(s_att, g - 1)
            for which in range(2):
                for half in range(2):
                    for q in range(4):
                        last = nc.tensor.matmul(banks[g % 2 * 2 + which][32 * q:32 * q + 32, half, :],
                                                pick[:, which, :], oT[:, 4 * g + q, half * HALF:(half + 1) * HALF],
                                                start=True, stop=True)
            last.then_inc(s_u, 1)
        pe.wait_ge(s_ld[0], 32)
        pe.wait_ge(s_att, 4)

        def turn(qt):
            pe.wait_ge(s_x1, qt + 1)
            if qt >= 2:
                pe.wait_ge(s_x1T, qt - 1)
            for c in range(DC):
                last = nc.tensor.transpose(banks[2 + qt % 2][:, 0, c * P:(c + 1) * P], x1[:, qt, c * P:(c + 1) * P],
                                           ident[:, :])
            last.then_inc(s_tr, 1)

        for qt in range(QT):
            if qt >= 2:
                pe.wait_ge(s_sum, qt - 1)
            for g in range(4):
                last = nc.tensor.matmul(banks[qt % 2][:, 0, 0:D], att[:, g, qt * P:(qt + 1) * P], woT[:, g, :],
                                        start=(g == 0), stop=(g == 3))
            last.then_inc(s_proj, 1)
        for qt in range(QT):
            turn(qt)
        pe.wait_ge(s_ld[2], 16)
        pe.wait_ge(s_x1T, QT)
        for n in range(4 * E1):
            e, f, half = n // 4, n // 2 % 2, n % 2
            pe.wait_ge(s_xm, 2 * (e + 1))
            if n >= 4:
                pe.wait_ge(s_h, n - 3)
            for c in range(DC):
                last = nc.tensor.matmul(banks[n % 4][:, 0, :], ctxT[:, e, c, f * P:(f + 1) * P],
                                        xm[:, e % 2, c, half * HALF:(half + 1) * HALF], start=(c == 0), stop=(c == DC - 1))
            last.then_inc(s_z, 1)
        pe.wait_ge(s_h, 4 * E1)
        for qt in range(QT):
            if qt >= 2:
                pe.wait_ge(s_sum, QT + qt - 1)
            for e in range(E1):
                for f in range(2):
                    last = nc.tensor.matmul(banks[qt % 2][:, 0, 0:D], hid[:, e, f, qt * P:(qt + 1) * P],
                                            ctxT[:, e, f, :], start=(e == 0 and f == 0), stop=(e == E1 - 1 and f == 1))
            last.then_inc(s_y, 1)


NE, FFN, TOPK = 64, 176, 6
FC = FFN // 2
SFC = 2 * FFN // FC


def mixture(nc, ctx, a, x2, out):
    sb = lambda name, shape, dt: ctx.enter_context(nc.sbuf_tensor(name, shape, dt))
    sem = lambda name: ctx.enter_context(nc.semaphore(name))

    gateT = sb("gateT", [P, DC, NE], F32)
    ident = sb("ident3", [P, P], F32)
    iota = sb("iota", [P, NE], F32)
    x2T = sb("x2T", [P, DC, T], F32)
    logits = sb("logits", [P, QT, NE], F32)
    red = sb("red", [P, 4, QT], F32)
    scores = sb("scores", [P, QT, NE], F32)
    top = sb("top", [P, QT, 8], F32)
    topi = sb("topi", [P, QT, 8], U32)
    topf = sb("topf", [P, QT, 8], F32)
    wt = sb("wt", [P, QT, TOPK], F32)
    eq = sb("eq", [P, QT, NE], F32)
    comb = sb("comb", [P, QT, NE], F32)
    wgu = [sb(f"wgu{b}", [P, DC, 4 * FC], F32) for b in range(2)]
    wd = [sb(f"wd{b}", [FC, 2, D], F32) for b in range(2)]
    silu = sb("silu3", [FC, 2, HALF], F32)
    hid = [sb(f"hid{b}", [FC, 2, HALF], F32) for b in range(2)]
    acc = sb("acc", [P, QT, D], F32)
    stats = sb("stats3", [P, QT, 6], F32)
    mv = sb("mv3", [P, QT, 2], F32)
    var = sb("var3", [P, QT], F32)
    std = sb("std3", [P, QT], F32)
    rstd = sb("rstd3", [P, QT], F32)
    gu = ctx.enter_context(nc.psum_tensor("gu", [P, 4, HALF], F32))
    dn = [ctx.enter_context(nc.psum_tensor(f"dn{b}", [P, 4, D], F32)) for b in range(2)]

    s_ld, s_c, s_po, s_ch, s_tr, s_x2T, s_lg, s_sub, s_ex, s_w, s_gu, s_si, s_h, s_dn, s_acc, s_var, s_std, s_y, s_out = (
        sem("m_" + n) for n in "ld c po ch tr x2T lg sub ex w gu si h dn acc var std y out".split())
    s_we = [sem(f"m_we{b}") for b in range(2)]
    NX = NE + 2

    block = ctx.enter_context(nc.Block())

    @block.sync
    def _(sp):
        sp.dma_start(gateT[:, :, :], a["gateT"]).then_inc(s_ld, 16)

        def load(e, b):
            sp.dma_start(wgu[b][:, :, :].rearrange("p c f -> p (c f)"),
                         a["wgu"][bass.ds(e, 1), :, :].rearrange("o p n -> p (o n)")).then_inc(s_we[b], 16)
            sp.dma_start(wd[b][:, :, :].rearrange("p c f -> p (c f)"),
                         a["wd"][bass.ds(e, 1), :, :].rearrange("o p n -> p (o n)")).then_inc(s_we[b], 16)

        load(0, 0)
        load(1, 1)
        with sp.Fori(1, NX // 2) as i:
            for b in range(2):
                sp.wait_ge(s_dn, 2 * (2 * i + b - 1))
                load(2 * i + b, b)
        sp.wait_ge(s_y, QT)
        sp.dma_start(out, acc[:, :, :]).then_inc(s_out, 16)
        sp.wait_ge(s_out, 16)

    @block.gpsimd
    def _(pool):
        order = [0]

        def link(ins):
            order[0] += 1
            ins.then_inc(s_po, 1)
            pool.wait_ge(s_po, order[0])

        link(nc.gpsimd.memset(ident[:, :], 0.0))
        link(nc.gpsimd.affine_select(out=ident[:, :], in_=ident[:, :], compare_op=ALU.not_equal, fill=1.0, base=0,
                                     pattern=[[-1, P]], channel_multiplier=1))
        link(nc.gpsimd.iota(iota[:, :], [[1, NE]], base=0, channel_multiplier=0, allow_small_or_imprecise_dtypes=True))
        pool.sem_inc(s_c, 1)

    @block.scalar
    def _(act):
        for qt in range(QT):
            act.wait_ge(s_tr, qt + 1)
            nc.scalar.activation(x2T[:, :, qt * P:(qt + 1) * P], gu[:, qt % 4, 0:D]
                                 .rearrange("p (c n) -> p c n", c=DC), ACT.Copy).then_inc(s_x2T, 1)
        act.wait_ge(s_sub, 1)
        nc.scalar.activation(scores[:, :, :], logits[:, :, :], ACT.Exp).then_inc(s_ex, 1)

        with act.Fori(0, NX // 2) as i:
            for u in range(4):
                n = 4 * i + u
                act.wait_ge(s_gu, n + 1)
                act.wait_ge(s_h, n + 1)
                nc.scalar.activation(silu[:, :, :], gu[0:FC, 0:2, :], ACT.Silu).then_inc(s_si, 1)
        act.wait_ge(s_var, 1)
        nc.scalar.activation(std[:, :], var[:, :], ACT.Sqrt).then_inc(s_std, 1)

    @block.vector
    def _(dve):
        order = [0]

        def link(ins):
            order[0] += 1
            ins.then_inc(s_ch, 1)
            dve.wait_ge(s_ch, order[0])

        spread = lambda v: v.rearrange("p (q o) -> p q o", o=1).broadcast_to([P, QT, NE])
        dve.wait_ge(s_c, 1)
        dve.wait_ge(s_lg, 1)
        lg = dn[0][:, 0:2, :].rearrange("p a (b e) -> p (a b) e", e=NE)
        link(nc.vector.tensor_reduce(red[:, 0, :], lg, AX.X, ALU.max))
        nc.vector.tensor_tensor(logits[:, :, :], lg, spread(red[:, 0, :]), ALU.subtract).then_inc(s_sub, 1)
        dve.wait_ge(s_ex, 1)
        link(nc.vector.tensor_reduce(red[:, 1, :], scores[:, :, :], AX.X, ALU.add))
        link(nc.vector.reciprocal(red[:, 2, :], red[:, 1, :]))
        link(nc.vector.tensor_tensor(scores[:, :, :], scores[:, :, :], spread(red[:, 2, :]), ALU.mult))
        for qt in range(QT):
            link(nc.vector.max(top[:, qt, :], scores[:, qt, :]))
            link(nc.vector.max_index(topi[:, qt, :], top[:, qt, :], scores[:, qt, :]))
        link(nc.vector.tensor_copy(topf[:, :, :], topi[:, :, :]))
        link(nc.vector.tensor_reduce(red[:, 0, :], top[:, :, 0:TOPK], AX.X, ALU.add))
        link(nc.vector.tensor_scalar(red[:, 1, :], red[:, 0, :], 1e-20, None, ALU.add))
        link(nc.vector.reciprocal(red[:, 3, :], red[:, 1, :]))
        link(nc.vector.tensor_tensor(wt[:, :, :], top[:, :, 0:TOPK],
                                     red[:, 3, :].rearrange("p (q o) -> p q o", o=1).broadcast_to([P, QT, TOPK]), ALU.mult))
        link(nc.vector.memset(comb[:, :, :], 0.0))
        experts = iota[:, :].rearrange("p (o e) -> p o e", o=1).broadcast_to([P, QT, NE])
        for j in range(TOPK):
            link(nc.vector.tensor_tensor(eq[:, :, :], experts, spread(topf[:, :, j]), ALU.is_equal))
            link(nc.vector.tensor_tensor(eq[:, :, :], eq[:, :, :], spread(wt[:, :, j]), ALU.mult))
            link(nc.vector.tensor_tensor(comb[:, :, :], comb[:, :, :], eq[:, :, :], ALU.add))
        link(nc.vector.tensor_copy(acc[:, :, :], x2[:, :, :]))

        def expert(i, b, weight):
            for half in range(2):
                n = 4 * i + 2 * b + half
                dve.wait_ge(s_si, n + 1)
                nc.vector.tensor_tensor(hid[half][:, :, :], gu[0:FC, 2:4, :], silu[:, :, :], ALU.mult).then_inc(s_h, 1)
                dve.wait_ge(s_dn, n + 1)
                for q in range(4):
                    qt = 4 * half + q
                    nc.vector.scalar_tensor_tensor(out=acc[:, qt, :], in0=dn[half][:, q, :], scalar=weight(qt),
                                                   in1=acc[:, qt, :], op0=ALU.mult, op1=ALU.add).then_inc(s_acc, 1)
                dve.wait_ge(s_acc, 4 * (n + 1))

        with dve.Fori(0, NE // 2) as i:
            for b in range(2):
                expert(i, b, lambda qt: comb[:, qt, bass.ds(2 * i + b, 1)])
        for b in range(2):
            expert(NE // 2, b, lambda qt: 1.0)
        for qt in range(QT):
            link(nc.vector.bn_stats(stats[:, qt, :], acc[:, qt, :]))
            link(nc.vector.bn_aggr(mv[:, qt, :], stats[:, qt, :]))
        nc.vector.tensor_scalar(var[:, :], mv[:, :, 1], EPS, None, ALU.add).then_inc(s_var, 1)
        dve.wait_ge(s_std, 1)
        link(nc.vector.reciprocal(rstd[:, :], std[:, :]))
        for qt in range(QT):
            nc.vector.tensor_scalar(acc[:, qt, :], acc[:, qt, :], mv[:, qt, 0:1], rstd[:, qt:qt + 1], ALU.subtract,
                                    ALU.mult).then_inc(s_y, 1)

    @block.tensor
    def _(pe):
        pe.wait_ge(s_c, 1)
        for qt in range(QT):
            if qt >= 4:
                pe.wait_ge(s_x2T, qt - 3)
            for c in range(DC):
                last = nc.tensor.transpose(gu[:, qt % 4, c * P:(c + 1) * P], x2[:, qt, c * P:(c + 1) * P], ident[:, :])
            last.then_inc(s_tr, 1)
        pe.wait_ge(s_x2T, QT)
        pe.wait_ge(s_ld, 16)
        for qt in range(QT):
            for c in range(DC):
                last = nc.tensor.matmul(dn[0][:, qt // 4, (qt % 4) * NE:(qt % 4 + 1) * NE], x2T[:, c, qt * P:(qt + 1) * P],
                                        gateT[:, c, :], start=(c == 0), stop=(c == DC - 1))
        last.then_inc(s_lg, 1)
        pe.sem_inc(s_h, 1)
        pe.wait_ge(s_sub, 1)
        with pe.Fori(0, NX // 2) as i:
            for b in range(2):
                pe.wait_ge(s_we[b], 32 * (i + 1))
                for half in range(2):
                    n = 4 * i + 2 * b + half
                    pe.wait_ge(s_h, n + 1)
                    for f in range(4):
                        for c in range(DC):
                            last = nc.tensor.matmul(gu[0:FC, f, :], wgu[b][:, c, f * FC:(f + 1) * FC],
                                                    x2T[:, c, half * HALF:(half + 1) * HALF], start=(c == 0), stop=(c == DC - 1))
                    last.then_inc(s_gu, 1)
                    pe.wait_ge(s_h, n + 2)
                    for q in range(4):
                        for f in range(2):
                            last = nc.tensor.matmul(dn[half][:, q, :], hid[half][:, f, q * P:(q + 1) * P], wd[b][:, f, :],
                                                    start=(f == 0), stop=(f == 1))
                    last.then_inc(s_dn, 1)


def program(nc, a, out):
    with nc.sbuf_tensor("x2", [P, QT, D], F32) as x2:
        with nc.sbuf_tensor("oT", [P, HEADS, T], F32) as oT:
            with ExitStack() as ctx:
                attention(nc, ctx, a, oT)
            with ExitStack() as ctx:
                project_and_experts(nc, ctx, a, oT, x2)
        with ExitStack() as ctx:
            mixture(nc, ctx, a, x2, out)


def kernel(x, itok_BxS_13_99985, ctx_2048, L0_attn_kv_k, L0_attn_kv_v, L0_attn_Wq, L0_attn_Wo, L0_ffn_gate_w,
           L0_ffn_w_gate_up, L0_ffn_w_down, L0_ffn_ws_gate_up, L0_ffn_ws_down):
    import concourse.bacc as bacc
    from concourse.bass_utils import run_bass_kernel_spmd as run

    chunks = lambda m: np.ascontiguousarray(m.reshape(-1, P, m.shape[1]).transpose(1, 0, 2))
    xs = np.asarray(x).reshape(T, D)
    wo = np.asarray(L0_attn_Wo).T.reshape(4, 4, HD, D)
    wo_pad = np.zeros((4, 4, 32, D), wo.dtype)
    wo_pad[:, :, :HD] = wo
    arrays = {
        "x": chunks(xs),
        "xT": chunks(xs.T),
        "wqT": chunks(np.asarray(L0_attn_Wq).T),
        "woT": chunks(wo_pad.reshape(4 * P, D)),
        "kT": chunks(np.asarray(L0_attn_kv_k).reshape(KV, D).T),
        "v": np.ascontiguousarray(np.asarray(L0_attn_kv_v).reshape(KT, P, HEADS, HD).transpose(2, 1, 0, 3)
                                  .reshape(HEADS, P, KT * HD)),
        "ids": np.ascontiguousarray(np.asarray(itok_BxS_13_99985).reshape(T)),
        "ctxT": np.ascontiguousarray(np.asarray(ctx_2048).transpose(0, 2, 1).reshape(E1, DC, P, F1)
                                     .transpose(2, 0, 1, 3)),
    }
    gu = np.asarray(L0_ffn_w_gate_up)
    sgu = np.asarray(L0_ffn_ws_gate_up).reshape(2, 2, FFN, D).transpose(1, 0, 2, 3).reshape(2, 2 * FFN, D)
    gu = np.concatenate([gu, sgu]).transpose(0, 2, 1).reshape(NE + 2, DC, P, 2 * FFN).transpose(0, 2, 1, 3)
    dn = np.asarray(L0_ffn_w_down)
    sdn = np.asarray(L0_ffn_ws_down).reshape(D, 2, FFN).transpose(1, 0, 2)
    dn = np.concatenate([dn, sdn]).transpose(0, 2, 1).reshape(NE + 2, 2, FC, D).transpose(0, 2, 1, 3)
    arrays["wgu"] = np.ascontiguousarray(gu.reshape(NE + 2, P, DC * 2 * FFN))
    arrays["wd"] = np.ascontiguousarray(dn.reshape(NE + 2, FC, 2 * D))
    arrays["gateT"] = chunks(np.asarray(L0_ffn_gate_w).T)
    nc = bacc.Bacc("TRN2", target_bir_lowering=False, num_devices=1)
    a = {n: nc.dram_tensor(n + "_in", v.shape, mybir.dt.from_np(v.dtype), kind="ExternalInput").ap()
         for n, v in arrays.items()}
    out = nc.dram_tensor("out", (P, QT, D), F32, kind="ExternalOutput").ap()
    program(nc, a, out)
    r = run(nc, [{n + "_in": v for n, v in arrays.items()}], core_ids=[0])
    return np.ascontiguousarray(r.results[0]["out"].transpose(1, 0, 2)).reshape(4, 256, D)
```

```python
import numpy as np
import concourse.bass as bass
from concourse import mybir
from contextlib import ExitStack

F32 = mybir.dt.float32
BF16 = mybir.dt.bfloat16
I32 = mybir.dt.int32
U32 = mybir.dt.uint32
ALU = mybir.AluOpType
ACT = mybir.ActivationFunctionType
AX = mybir.AxisListType

P = 128
T, D = 1024, 256
DC = D // P
QT = T // P
HEADS, HD = 16, 16
KV = 4096
KT = KV // P
SCALE = 1.0 / 4.0
EPS = 1e-5

GROUPS = [(0, 0), (0, 1), (1, 0), (1, 1), (2, 0), (0, 2)]
ROWS = len(GROUPS) * HD
MROWS = 3
RING = 4
AHEAD = 3
HALF = 512
PAIRS = QT * KV // 1024
FIRST_PAIRS = 4
STEPS = 2 * KT
SG = KT // 4
CH = 1024

ZT = 2
E1 = 4
F1 = 256
VOCAB = 12500


def attention(nc, ctx, a, oT, xs):
    sb = lambda name, shape, dt: ctx.enter_context(nc.sbuf_tensor(name, shape, dt))
    pb = lambda name, shape: ctx.enter_context(nc.psum_tensor(name, shape, F32))
    sem = lambda name: ctx.enter_context(nc.semaphore(name))

    flat = oT[:, :, :].rearrange("p h t -> p (h t)")
    taken = [0]

    def early(*shape):
        size = int(np.prod(shape))
        view = flat[:, taken[0]:taken[0] + size]
        taken[0] += size
        if len(shape) > 1:
            view = view.rearrange("p (a n) -> p a n", a=shape[0])
        return view

    def early_bf16(*shape):
        size = int(np.prod(shape))
        view = flat[:, taken[0]:taken[0] + size // 2].bitcast(BF16)
        taken[0] += size // 2
        names = {2: ("p (a n) -> p a n", {"a": shape[0]}),
                 3: ("p (a b n) -> p a b n", {"a": shape[0], "b": shape[1] if len(shape) > 2 else 1})}
        return view.rearrange(names[len(shape)][0], **names[len(shape)][1])

    xT = early(DC, T)
    wqT = early(DC, D)
    kstack = [sb(f"kstack{b}", [ROWS + MROWS, KV], BF16) for b in range(RING)]
    qstack = [sb(f"qstack{b}", [ROWS + MROWS, T], BF16) for b in range(RING)]
    ksrc = [[early(CH) for i in range(2)], [sb(f"ksrc{i}", [P, CH], F32) for i in range(2)]]
    kres = [[early(CH) for i in range(2)], [sb(f"kres{i}", [P, CH], F32) for i in range(2)]]
    kpart = [[early_bf16(3, CH) for i in range(2)], [sb(f"kpart{i}", [P, 3, CH], BF16) for i in range(2)]]
    qpart = early_bf16(4, 3, HALF)
    qres = kres[0][0]
    vstage = [sb(f"vstage{b}", [P, KT, HD], F32) for b in range(2)]
    vpad = [sb(f"vpad{b}", [P, KT, 32], F32) for b in range(2)]
    ones = sb("ones", [P, KT, HD], F32)
    weights = sb("weights", [P, 2, 4, T], F32)
    mx4 = sb("mx4", [P, QT, 4], F32)
    mneg = sb("mneg", [P, QT], F32)
    mres = sb("mres", [P, QT], F32)
    mres2 = sb("mres2", [P, QT], F32)
    m3 = sb("m3", [P, QT, 3], BF16)
    ident = sb("ident_bf", [P, P], BF16)
    zero = sb("zero", [P, ZT * D], F32)

    Mb = pb("Mb", [P, 2, 1024])
    Sb = pb("Sb", [P, 2, HALF])
    Ob = pb("Ob", [P, 2, HALF])
    Qb = Mb[:, :, :].rearrange("p a (b n) -> p (a b) n", b=2)

    kparts = nc.dram_tensor("kparts", [3, D, KV], BF16, kind="Internal").ap()
    qparts = nc.dram_tensor("qparts", [3, D, T], BF16, kind="Internal").ap()

    s_x = sem("s_x")
    s_ksrc = [sem(f"s_ksrc{c}{i}") for c in range(DC) for i in range(2)]
    s_q = sem("s_q")
    s_qc = sem("s_qc")
    s_qs = sem("s_qs")
    s_kc = sem("s_kc")
    s_ks = sem("s_ks")
    s_kp = sem("s_kp")
    s_kpo = sem("s_kpo")
    s_qw = sem("s_qw")
    s_kw = [[sem(f"s_kw{c}{i}") for i in range(2)] for c in range(DC)]
    s_zero = sem("s_zero")
    s_zf = sem("s_zf")
    s_const = sem("s_const")
    s_stack = [sem(f"s_stack{b}") for b in range(RING)]
    s_vload = [sem(f"s_vload{b}") for b in range(2)]
    s_v = sem("s_v")
    s_mx = sem("s_mx")
    s_mred = sem("s_mred")
    s_mch = sem("s_mch")
    s_m3 = sem("s_m3")
    s_mt = sem("s_mt")
    s_qm = sem("s_qm")
    s_st = sem("s_st")
    s_exp = sem("s_exp")
    s_pv = sem("s_pv")
    s_ot = sem("s_ot")

    block = ctx.enter_context(nc.Block())
    NCH = KV // CH
    LOADED = 2 * len(GROUPS) * 16

    @block.sync
    def _(sp):
        def load_chunk(c, i):
            if i >= 2:
                if c == 0:
                    sp.wait_ge(s_ks, 2 * (i - 1))
                else:
                    sp.wait_ge(s_kp, i - 1)
            sp.dma_start(ksrc[c][i % 2][:, :], a["kT"][:, c, i * CH:(i + 1) * CH]).then_inc(s_ksrc[2 * c + i % 2], 16)

        def store_chunk(c, i):
            if c == 0:
                sp.wait_ge(s_ks, 2 * (i + 1))
            else:
                sp.wait_ge(s_kp, i + 1)
            for part in range(3):
                sp.dma_start(kparts[part, c * P:(c + 1) * P, i * CH:(i + 1) * CH],
                             kpart[c][i % 2][:, part, :]).then_inc(s_kw[c][i % 2], 16)

        def load_stack(h, b):
            for g, (kp, qp) in enumerate(GROUPS):
                rows = slice(g * HD, (g + 1) * HD)
                sp.dma_start(kstack[b][rows, :], kparts[kp, bass.ds(h * HD, HD), :]).then_inc(s_stack[b], 16)
                sp.dma_start(qstack[b][rows, :], qparts[qp, bass.ds(h * HD, HD), :]).then_inc(s_stack[b], 16)

        def load_v(h, b):
            sp.dma_start(vstage[b][:, :, :], a["v"][bass.ds(h, 1), :, :].rearrange("o p n -> p (o n)")
                         .rearrange("p (k d) -> p k d", k=KT)).then_inc(s_vload[b], 16)

        sp.dma_start(wqT[:, :, :], a["wqT"]).then_inc(s_x, 16)
        sp.dma_start(xT[:, :, :], a["xT"]).then_inc(s_x, 16)
        for i in range(2):
            load_chunk(0, i)
        for i in range(NCH):
            if i + 2 < NCH:
                load_chunk(0, i + 2)
            store_chunk(0, i)
        load_v(0, 0)
        for n in range(4):
            sp.wait_ge(s_qs, 2 * (n + 1))
            c, half = n // 2, n % 2
            for part in range(3):
                sp.dma_start(qparts[part, c * P:(c + 1) * P, half * HALF:(half + 1) * HALF],
                             qpart[:, n, part, :]).then_inc(s_qw, 16)
        sp.wait_ge(s_qw, 12 * 16)
        for i in range(2):
            sp.wait_ge(s_kw[0][i], 3 * 16 * (NCH // 2))
        for h in range(AHEAD):
            load_stack(h, h)
        for i in range(2):
            load_chunk(1, i)
        for i in range(NCH):
            if i + 2 < NCH:
                load_chunk(1, i + 2)
            store_chunk(1, i)
        for i in range(2):
            sp.wait_ge(s_kw[1][i], 3 * 16 * (NCH // 2))

        def head(h, b, stack, v):
            if v:
                sp.wait_ge(s_v, h)
                load_v(h + 1, (b + 1) % 2)
            if stack:
                sp.wait_ge(s_st, h * STEPS)
                sp.wait_ge(s_qm, h)
                load_stack(h + AHEAD, (b + AHEAD) % RING)

        load_v(1, 1)
        load_stack(AHEAD, AHEAD)
        sp.wait_ge(s_zero, 1)
        for n in range(TILES // ZT):
            sp.dma_start(xs[n * ZT * P:(n + 1) * ZT * P, :].rearrange("(p r) d -> p (r d)", r=ZT), zero[:, :]
                         ).then_inc(s_zf, 16)
        for h in range(1, RING):
            head(h, h, True, True)
        with sp.Fori(1, HEADS // RING - 1) as i:
            for b in range(RING):
                head(RING * i + b, b, True, True)
        for h in range(HEADS - RING, HEADS):
            head(h, h % RING, h + AHEAD < HEADS, h + 1 < HEADS)
        sp.wait_ge(s_zf, 16 * (TILES // ZT))

    @block.gpsimd
    def _(pool):
        order = [0]

        def link(ins):
            order[0] += 1
            ins.then_inc(s_kpo, 1)
            pool.wait_ge(s_kpo, order[0])

        link(nc.gpsimd.memset(ident[:, :], 0.0))
        link(nc.gpsimd.affine_select(out=ident[:, :], in_=ident[:, :], compare_op=ALU.not_equal, fill=1.0, base=0,
                                     pattern=[[-1, P]], channel_multiplier=1))
        pool.sem_inc(s_const, 1)
        link(nc.gpsimd.memset(ones[:, :, :], 1.0))
        for b in range(2):
            link(nc.gpsimd.memset(vpad[b][:, :, HD:32], 0.0))
            link(nc.gpsimd.memset(vpad[b][:, :, HD:HD + 1], 1.0))

        def pad_v(h, b, nth, waits):
            pool.wait_ge(s_vload[b], 16 * nth)
            if waits:
                pool.wait_ge(s_pv, 4 + (h - 1) * 2 * SG)
                pool.wait_ge(s_v, h)
            nc.gpsimd.tensor_tensor(vpad[b][:, :, 0:HD], vstage[b][:, :, :], ones[:, :, :],
                                    ALU.mult).then_inc(s_v, 1)

        pad_v(0, 0, 1, False)
        pool.wait_ge(s_v, 1)
        for i in range(NCH):
            pool.wait_ge(s_ksrc[2 + i % 2], 16 * (i // 2 + 1))
            if i >= 2:
                pool.wait_ge(s_kw[1][i % 2], 48 * (i // 2))
            src, res, part = ksrc[1][i % 2], kres[1][i % 2], kpart[1][i % 2]
            link(nc.gpsimd.tensor_copy(part[:, 0, :], src[:, :]))
            link(nc.gpsimd.tensor_tensor(res[:, :], src[:, :], part[:, 0, :], ALU.subtract))
            link(nc.gpsimd.tensor_copy(part[:, 1, :], res[:, :]))
            nc.gpsimd.tensor_tensor(part[:, 2, :], res[:, :], part[:, 1, :], ALU.subtract).then_inc(s_kp, 1)
            pool.wait_ge(s_kp, i + 1)
        pad_v(1, 1, 1, False)
        for h in range(2, RING):
            pad_v(h, h % 2, h // 2 + 1, True)
        with pool.Fori(1, HEADS // RING) as i:
            for b in range(RING):
                pad_v(RING * i + b, b % 2, 2 * i + b // 2 + 1, True)

    @block.scalar
    def _(act):
        for n in range(4):
            act.wait_ge(s_q, n + 1)
            nc.scalar.activation(qpart[:, n, 0, :], Qb[:, n, :], ACT.Copy).then_inc(s_qc, 1)
            act.wait_ge(s_qs, 2 * n + 1)
            nc.scalar.activation(qpart[:, n, 1, :], qres[:, (n % 2) * HALF:(n % 2 + 1) * HALF],
                                 ACT.Copy).then_inc(s_qc, 1)
        for i in range(NCH):
            act.wait_ge(s_ksrc[i % 2], 16 * (i // 2 + 1))
            if i >= 2:
                act.wait_ge(s_kw[0][i % 2], 48 * (i // 2))
            nc.scalar.activation(kpart[0][i % 2][:, 0, :], ksrc[0][i % 2][:, :], ACT.Copy).then_inc(s_kc, 1)
            act.wait_ge(s_ks, 2 * i + 1)
            nc.scalar.activation(kpart[0][i % 2][:, 1, :], kres[0][i % 2][:, :], ACT.Copy).then_inc(s_kc, 1)

        def move_rows(h, b):
            act.wait_ge(s_mt, h + 1)
            nc.scalar.activation(qstack[b][ROWS:ROWS + MROWS, :], Sb[ROWS:ROWS + MROWS, :, :]
                                 .rearrange("p a n -> p (a n)"), ACT.Copy).then_inc(s_qm, 1)

        def head(h, b, last):
            for n in range(STEPS):
                kt, half = n // 2, n % 2
                s = kt // 4
                act.wait_ge(s_st, STEPS * h + n + 1)
                if n % 8 < 2:
                    act.wait_ge(s_pv, 2 * SG * h + 2 * s + half + 1)
                nc.scalar.activation(weights[:, s % 2, kt % 4, half * HALF:(half + 1) * HALF], Sb[:, n % 2, :],
                                     ACT.Exp, scale=SCALE).then_inc(s_exp, 1)
            if not last:
                move_rows(h + 1, (b + 1) % RING)
            act.wait_ge(s_pv, 4 + 2 * SG * (h + 1))
            nc.scalar.activation(oT[:, bass.ds(h, 1), :].rearrange("p o n -> p (o n)"),
                                 Ob[:, :, :].rearrange("p a n -> p (a n)"), ACT.Copy).then_inc(s_ot, 1)

        move_rows(0, 0)
        with act.Fori(0, HEADS // RING - 1) as i:
            for b in range(RING):
                head(RING * i + b, b, False)
        for h in range(HEADS - RING, HEADS):
            head(h, h % RING, h == HEADS - 1)

    @block.vector
    def _(dve):
        nc.vector.memset(zero[:, :], 0.0).then_inc(s_zero, 1)
        for b in range(RING):
            nc.vector.memset(kstack[b][ROWS:ROWS + MROWS, :], 1.0).then_inc(s_const, 1)
        for n in range(4):
            res = qres[:, (n % 2) * HALF:(n % 2 + 1) * HALF]
            dve.wait_ge(s_qc, 2 * n + 1)
            nc.vector.tensor_tensor(res, Qb[:, n, :], qpart[:, n, 0, :], ALU.subtract).then_inc(s_qs, 1)
            dve.wait_ge(s_qc, 2 * n + 2)
            dve.wait_ge(s_qs, 2 * n + 1)
            nc.vector.tensor_tensor(qpart[:, n, 2, :], res, qpart[:, n, 1, :], ALU.subtract).then_inc(s_qs, 1)
        dve.wait_ge(s_qs, 8)
        for i in range(NCH):
            src, res, part = ksrc[0][i % 2], kres[0][i % 2], kpart[0][i % 2]
            dve.wait_ge(s_kc, 2 * i + 1)
            nc.vector.tensor_tensor(res[:, :], src[:, :], part[:, 0, :], ALU.subtract).then_inc(s_ks, 1)
            dve.wait_ge(s_kc, 2 * i + 2)
            dve.wait_ge(s_ks, 2 * i + 1)
            nc.vector.tensor_tensor(part[:, 2, :], res[:, :], part[:, 1, :], ALU.subtract).then_inc(s_ks, 1)

        def link(ins, count):
            ins.then_inc(s_mch, 1)
            dve.wait_ge(s_mch, count)

        CHAIN = 5

        def maxima(h, first):
            for j in range(PAIRS):
                dve.wait_ge(s_mx, PAIRS * h + j + 1)
                nc.vector.tensor_reduce(mx4[:, j // 4, j % 4:j % 4 + 1], Mb[:, j % 2, :], AX.X,
                                        ALU.max).then_inc(s_mred, 1)
            dve.wait_ge(s_mred, PAIRS * (h + 1))
            if not first:
                dve.wait_ge(s_mt, h)
            n = CHAIN * h
            link(nc.vector.tensor_reduce(mres[:, :], mx4[:, :, :], AX.X, ALU.max), n + 1)
            link(nc.vector.tensor_scalar(mneg[:, :], mres[:, :], -1.0, None, ALU.mult), n + 2)
            link(nc.vector.tensor_copy(m3[:, :, 0], mneg[:, :]), n + 3)
            link(nc.vector.tensor_tensor(mres2[:, :], mneg[:, :], m3[:, :, 0], ALU.subtract), n + 4)
            link(nc.vector.tensor_copy(m3[:, :, 1], mres2[:, :]), n + 5)
            nc.vector.tensor_tensor(m3[:, :, 2], mres2[:, :], m3[:, :, 1], ALU.subtract).then_inc(s_m3, 1)

        maxima(0, True)
        with dve.Fori(0, HEADS // RING - 1) as i:
            for b in range(RING):
                maxima(RING * i + b + 1, False)
        for h in range(HEADS - RING + 1, HEADS):
            maxima(h, False)

    @block.tensor
    def _(pe):
        pe.wait_ge(s_x, 32)
        for n in range(4):
            c, half = n // 2, n % 2
            for k in range(DC):
                last = nc.tensor.matmul(Qb[:, n, :], wqT[:, k, c * P:(c + 1) * P],
                                        xT[:, k, half * HALF:(half + 1) * HALF], start=(k == 0), stop=(k == DC - 1))
            last.then_inc(s_q, 1)

        def pair(h, b, j, prologue):
            if not (prologue and j < 2):
                pe.wait_ge(s_mred, PAIRS * h + j - 1)
            qt, kc = j // 4, j % 4
            for u in range(2):
                k0 = kc * 1024 + u * HALF
                last = nc.tensor.matmul(Mb[:, j % 2, u * HALF:(u + 1) * HALF], qstack[b][0:ROWS, qt * P:(qt + 1) * P],
                                        kstack[b][0:ROWS, k0:k0 + HALF], start=True, stop=True)
            last.then_inc(s_mx, 1)

        def max_rows(h):
            pe.wait_ge(s_m3, h + 1)
            for qt in range(QT):
                last = nc.tensor.matmul(Sb[ROWS:ROWS + MROWS, qt // 4, (qt % 4) * P:(qt % 4 + 1) * P], m3[:, qt, :],
                                        ident[:, :], start=True, stop=True)
            last.then_inc(s_mt, 1)

        def weigh(h, b, s, half):
            if s == 0 and half == 0:
                pe.wait_ge(s_v, h + 1)
                pe.wait_ge(s_ot, h + 1)
            pe.wait_ge(s_exp, STEPS * h + 8 * s + 7 + half)
            for g in range(4):
                last = nc.tensor.matmul(Ob[32 * g:32 * g + 32, half, :], vpad[b % 2][:, 4 * s + g, :],
                                        weights[:, s % 2, g, half * HALF:(half + 1) * HALF],
                                        start=(s == 0), stop=(s == SG - 1))
            last.then_inc(s_pv, 1)

        def head(h, b, last):
            nb = (b + 1) % RING
            for j in range(0 if last else FIRST_PAIRS):
                pair(h + 1, nb, j, False)
            pe.wait_ge(s_qm, h + 1)
            for n in range(STEPS):
                kt, half = n // 2, n % 2
                if n >= 2:
                    pe.wait_ge(s_exp, STEPS * h + n - 1)
                nc.tensor.matmul(Sb[:, n % 2, :], kstack[b][:, kt * P:(kt + 1) * P],
                                 qstack[b][:, half * HALF:(half + 1) * HALF], start=True, stop=True).then_inc(s_st, 1)
                if half == 1 and not last and kt + FIRST_PAIRS < PAIRS:
                    pair(h + 1, nb, kt + FIRST_PAIRS, False)
                if n % 4 == 3 and kt >= 4:
                    weigh(h, b, kt // 4 - 1, kt % 4 // 2)
            if not last:
                pe.wait_ge(s_exp, STEPS * (h + 1))
                max_rows(h + 1)
            for half in range(2):
                weigh(h, b, SG - 1, half)

        pe.wait_ge(s_qs, 8)
        pe.wait_ge(s_const, 1 + RING)
        pe.wait_ge(s_stack[0], LOADED)
        for j in range(PAIRS):
            pair(0, 0, j, True)
        max_rows(0)
        pe.sem_inc(s_pv, 4)
        pe.sem_inc(s_ot, 1)

        with pe.Fori(0, HEADS // RING - 1) as i:
            for b in range(RING):
                pe.wait_ge(s_stack[(b + 1) % RING], LOADED * (i + 1 + (b + 1) // RING))
                head(RING * i + b, b, False)
        for h in range(HEADS - RING, HEADS):
            if h + 1 < HEADS:
                pe.wait_ge(s_stack[(h + 1) % RING], LOADED * ((h + 1) // RING + 1))
            head(h, h % RING, h == HEADS - 1)


def project_and_experts(nc, ctx, a, oT, x2):
    sb = lambda name, shape, dt: ctx.enter_context(nc.sbuf_tensor(name, shape, dt))
    sem = lambda name: ctx.enter_context(nc.semaphore(name))
    banks = [ctx.enter_context(nc.psum_tensor(f"bank{i}", [P, 2, HALF], F32)) for i in range(4)]

    x = sb("x", [P, QT, D], F32)
    woT = sb("woT", [P, 4, D], F32)
    ctxT = sb("ctxT", [P, E1, DC, F1], F32)
    ids = sb("ids", [P, T], I32)
    idf = sb("idf", [P, T], F32)
    ge = sb("ge", [P, 3, T], F32)
    mask = sb("mask", [P, E1, T], F32)
    ident = sb("ident", [P, P], F32)
    pick = sb("pick", [P, 2, 32], F32)
    att = sb("att", [P, 4, T], F32)
    rden = sb("rden", [P, T], F32)
    stats = sb("stats", [P, QT, 6], F32)
    mv = sb("mv", [P, QT, 2], F32)
    var = sb("var", [P, QT], F32)
    std = sb("std", [P, QT], F32)
    rstd = sb("rstd", [P, QT], F32)
    x1 = sb("x1", [P, QT, D], F32)
    x1T = sb("x1T", [P, DC, T], F32)
    xm = sb("xm", [P, 2, DC, T], F32)
    silu = sb("silu", [P, 2, HALF], F32)
    hid = oT[:, 0:E1 * 2, :].rearrange("p (e f) t -> p e f t", f=2)

    s_ld = [sem(f"s_ld{i}") for i in range(4)]
    s_c = sem("s_c")
    s_po = sem("s_po")
    s_mask = sem("s_mask")
    s_u = sem("s_u")
    s_dch = sem("s_dch")
    s_att = sem("s_att")
    s_proj = sem("s_proj")
    s_x1 = sem("s_x1")
    s_tr = sem("s_tr")
    s_x1T = sem("s_x1T")
    s_xm = sem("s_xm")
    s_z = sem("s_z")
    s_si = sem("s_si")
    s_h = sem("s_h")
    s_y = sem("s_y")
    s_x2 = sem("s_x2")
    s_sum = sem("s_sum")
    s_var = sem("s_var")
    s_std = sem("s_std")

    block = ctx.enter_context(nc.Block())

    @block.sync
    def _(sp):
        sp.dma_start(woT[:, :, :], a["woT"]).then_inc(s_ld[0], 16)
        sp.dma_start(x[:, :, :], a["x"]).then_inc(s_ld[0], 16)
        sp.dma_start(ids[:, :], a["ids"].rearrange("(o t) -> o t", o=1).partition_broadcast(P)
                     if False else a["ids"].rearrange("(o t) -> o t", o=1).broadcast_to([P, T])).then_inc(s_ld[1], 16)
        sp.dma_start(ctxT[:, :, :, :], a["ctxT"]).then_inc(s_ld[2], 16)

    @block.gpsimd
    def _(pool):
        order = [0]

        def link(ins):
            order[0] += 1
            ins.then_inc(s_po, 1)
            pool.wait_ge(s_po, order[0])

        link(nc.gpsimd.memset(pick[:, :, :], 0.0))
        for g in range(4):
            link(nc.gpsimd.affine_select(out=pick[:, 0, :], in_=pick[:, 0, :], compare_op=ALU.not_equal, fill=1.0,
                                         base=-32 * g, pattern=[[-1, 32]], channel_multiplier=1))
            link(nc.gpsimd.affine_select(out=pick[:, 1, :], in_=pick[:, 1, :], compare_op=ALU.not_equal, fill=1.0,
                                         base=-32 * g - HD, pattern=[[0, 32]], channel_multiplier=1))
        link(nc.gpsimd.memset(ident[:, :], 0.0))
        link(nc.gpsimd.affine_select(out=ident[:, :], in_=ident[:, :], compare_op=ALU.not_equal, fill=1.0, base=0,
                                     pattern=[[-1, P]], channel_multiplier=1))
        pool.sem_inc(s_c, 1)
        pool.wait_ge(s_ld[1], 16)
        link(nc.gpsimd.tensor_copy(idf[:, :], ids[:, :]))
        for e in range(3):
            link(nc.gpsimd.tensor_scalar(ge[:, e, :], idf[:, :], float((e + 1) * (VOCAB // E1)), None, ALU.is_ge))
        link(nc.gpsimd.tensor_scalar(mask[:, 0, :], ge[:, 0, :], -1.0, 1.0, ALU.mult, ALU.add))
        for e in range(1, 3):
            link(nc.gpsimd.tensor_tensor(mask[:, e, :], ge[:, e - 1, :], ge[:, e, :], ALU.subtract))
        link(nc.gpsimd.tensor_copy(mask[:, 3, :], ge[:, 2, :]))
        pool.wait_ge(s_x1T, QT)
        for e in range(E1):
            if e >= 2:
                pool.wait_ge(s_z, 4 * (e - 1))
            for c in range(DC):
                nc.gpsimd.tensor_tensor(xm[:, e % 2, c, :], x1T[:, c, :], mask[:, e, :], ALU.mult).then_inc(s_xm, 1)
                pool.wait_ge(s_xm, DC * e + c + 1)

    @block.scalar
    def _(act):
        def root(nth):
            act.wait_ge(s_var, nth)
            nc.scalar.activation(std[:, :], var[:, :], ACT.Sqrt).then_inc(s_std, 1)

        root(1)
        for qt in range(QT):
            act.wait_ge(s_tr, qt + 1)
            nc.scalar.activation(x1T[:, :, qt * P:(qt + 1) * P], banks[2 + qt % 2][:, 0, 0:D]
                                 .rearrange("p (c n) -> p c n", c=DC), ACT.Copy).then_inc(s_x1T, 1)
        for n in range(4 * E1):
            act.wait_ge(s_z, n + 1)
            if n >= 2:
                act.wait_ge(s_h, n - 1)
            nc.scalar.activation(silu[:, n % 2, :], banks[n % 4][:, 0, :], ACT.Silu).then_inc(s_si, 1)
        root(2)

    @block.vector
    def _(dve):
        order = [0]

        def link(ins):
            order[0] += 1
            ins.then_inc(s_dch, 1)
            dve.wait_ge(s_dch, order[0])

        for g in range(4):
            dve.wait_ge(s_u, g + 1)
            sums, dens = banks[g % 2 * 2], banks[g % 2 * 2 + 1]
            link(nc.vector.reciprocal(rden[:, :], dens[:, :, :].rearrange("p a n -> p (a n)")))
            nc.vector.tensor_tensor(att[:, g, :], sums[:, :, :].rearrange("p a n -> p (a n)"), rden[:, :],
                                    ALU.mult).then_inc(s_att, 1)
            dve.wait_ge(s_att, g + 1)

        def statistics(qt, bank, base):
            nc.vector.tensor_tensor(base, bank, base, ALU.add).then_inc(s_sum, 1)
            sums[0] += 1
            dve.wait_ge(s_sum, sums[0])
            link(nc.vector.bn_stats(stats[:, qt, :], base))
            link(nc.vector.bn_aggr(mv[:, qt, :], stats[:, qt, :]))

        def deviations(nth):
            nc.vector.tensor_scalar(var[:, :], mv[:, :, 1], EPS, None, ALU.add).then_inc(s_var, 1)
            dve.wait_ge(s_std, nth)
            link(nc.vector.reciprocal(rstd[:, :], std[:, :]))

        def normalise(qt, out, base, done):
            nc.vector.tensor_scalar(out, base, mv[:, qt, 0:1], rstd[:, qt:qt + 1], ALU.subtract,
                                    ALU.mult).then_inc(done, 1)

        sums = [0]
        dve.wait_ge(s_ld[0], 32)
        for qt in range(QT):
            dve.wait_ge(s_proj, qt + 1)
            statistics(qt, banks[qt % 2][:, 0, 0:D], x[:, qt, :])
        deviations(1)
        for qt in range(QT):
            normalise(qt, x1[:, qt, :], x[:, qt, :], s_x1)
        for n in range(4 * E1):
            e, f, half = n // 4, n // 2 % 2, n % 2
            dve.wait_ge(s_si, n + 1)
            nc.vector.tensor_tensor(hid[:, e, f, half * HALF:(half + 1) * HALF], banks[n % 4][:, 0, :],
                                    silu[:, n % 2, :], ALU.mult).then_inc(s_h, 1)
        dve.wait_ge(s_x1, QT)
        for qt in range(QT):
            dve.wait_ge(s_y, qt + 1)
            statistics(qt, banks[qt % 2][:, 0, 0:D], x1[:, qt, :])
        deviations(2)
        for qt in range(QT):
            normalise(qt, x2[:, qt, :], x1[:, qt, :], s_x2)

    @block.tensor
    def _(pe):
        pe.wait_ge(s_c, 1)
        for g in range(4):
            if g >= 2:
                pe.wait_ge(s_att, g - 1)
            for which in range(2):
                for half in range(2):
                    for q in range(4):
                        last = nc.tensor.matmul(banks[g % 2 * 2 + which][32 * q:32 * q + 32, half, :],
                                                pick[:, which, :], oT[:, 4 * g + q, half * HALF:(half + 1) * HALF],
                                                start=True, stop=True)
            last.then_inc(s_u, 1)
        pe.wait_ge(s_ld[0], 32)
        pe.wait_ge(s_att, 4)

        def turn(qt):
            pe.wait_ge(s_x1, qt + 1)
            if qt >= 2:
                pe.wait_ge(s_x1T, qt - 1)
            for c in range(DC):
                last = nc.tensor.transpose(banks[2 + qt % 2][:, 0, c * P:(c + 1) * P], x1[:, qt, c * P:(c + 1) * P],
                                           ident[:, :])
            last.then_inc(s_tr, 1)

        for qt in range(QT):
            if qt >= 2:
                pe.wait_ge(s_sum, qt - 1)
            for g in range(4):
                last = nc.tensor.matmul(banks[qt % 2][:, 0, 0:D], att[:, g, qt * P:(qt + 1) * P], woT[:, g, :],
                                        start=(g == 0), stop=(g == 3))
            last.then_inc(s_proj, 1)
        for qt in range(QT):
            turn(qt)
        pe.wait_ge(s_ld[2], 16)
        pe.wait_ge(s_x1T, QT)
        for n in range(4 * E1):
            e, f, half = n // 4, n // 2 % 2, n % 2
            pe.wait_ge(s_xm, 2 * (e + 1))
            if n >= 4:
                pe.wait_ge(s_h, n - 3)
            for c in range(DC):
                last = nc.tensor.matmul(banks[n % 4][:, 0, :], ctxT[:, e, c, f * P:(f + 1) * P],
                                        xm[:, e % 2, c, half * HALF:(half + 1) * HALF], start=(c == 0), stop=(c == DC - 1))
            last.then_inc(s_z, 1)
        pe.wait_ge(s_h, 4 * E1)
        for qt in range(QT):
            if qt >= 2:
                pe.wait_ge(s_sum, QT + qt - 1)
            for e in range(E1):
                for f in range(2):
                    last = nc.tensor.matmul(banks[qt % 2][:, 0, 0:D], hid[:, e, f, qt * P:(qt + 1) * P],
                                            ctxT[:, e, f, :], start=(e == 0 and f == 0), stop=(e == E1 - 1 and f == 1))
            last.then_inc(s_y, 1)


NE, FFN, TOPK = 64, 176, 6
FC = FFN // 2
SF = 2 * FFN
SFC = SF // FC
UNROLL = 4
TILES = -(-((T * TOPK + NE * (P - 1)) // P) // UNROLL) * UNROLL
PICKS = QT * TOPK
GRING = 8


def mixture(nc, ctx, a, x2, out, xs):
    sb = lambda name, shape, dt: ctx.enter_context(nc.sbuf_tensor(name, shape, dt))
    pb = lambda name, shape: ctx.enter_context(nc.psum_tensor(name, shape, F32))
    sem = lambda name: ctx.enter_context(nc.semaphore(name))

    gateT = sb("gateT", [P, DC, NE], F32)
    swgu = sb("swgu", [P, DC, 2 * SF], F32)
    swd = sb("swd", [FC, SFC, D], F32)
    ident = sb("ident3", [P, P], F32)
    iota = sb("iota", [P, P], F32)
    before = sb("before", [P, P], BF16)
    upto = sb("upto", [NE, NE], F32)
    onesb = sb("onesb", [P, P], BF16)
    onesf = sb("onesf", [P, NE], F32)
    x2T = sb("x2T", [P, DC, T], F32)
    logits = sb("logits", [P, QT, NE], F32)
    red = sb("red", [P, 4, QT], F32)
    scores = sb("scores", [P, QT, NE], F32)
    top = sb("top", [P, QT, 8], F32)
    topi = sb("topi", [P, QT, 8], U32)
    topf = sb("topf", [P, QT, 8], F32)
    wt = sb("wt", [P, TOPK, QT], F32)
    chosen = sb("chosen", [P, TOPK, QT, NE], F32)
    place = sb("place", [P, TOPK, QT, NE], F32)
    anyj = sb("anyj", [P, QT, NE], BF16)
    filled = sb("filled", [P, NE], I32)
    tilesi = sb("tilesi", [P, NE], I32)
    tiles = sb("tiles", [P, NE], F32)
    ends = sb("ends", [P, NE], F32)
    base = sb("base", [P, NE], F32)
    where = sb("where", [P, QT, NE], F32)
    slotf = sb("slotf", [P, PICKS], F32)
    slots = sb("slots", [P, PICKS], I32)
    cfill = sb("cfill", [NE, 1], I32)
    ctile = sb("ctile", [NE, 1], I32)
    ctilef = sb("ctilef", [NE, 1], F32)
    cend = sb("cend", [NE, 1], F32)
    past = sb("past", [NE, TILES], F32)
    owner = sb("owner", [1, TILES], I32)
    xg = [sb(f"xg{r}", [P, D], F32) for r in range(UNROLL)]
    wgu = [sb(f"wgu{r}", [P, DC * 2 * FFN], F32) for r in range(UNROLL)]
    wd = [sb(f"wd{r}", [FC, 2 * D], F32) for r in range(UNROLL)]
    yt = [sb(f"yt{r}", [P, D], F32) for r in range(UNROLL)]
    xgT = [sb(f"xgT{b}", [P, D], F32) for b in range(2)]
    silu = [sb(f"silu{b}", [P, FFN], F32) for b in range(2)]
    hid = [sb(f"hid{b}", [P, FFN], F32) for b in range(2)]
    hidT = [sb(f"hidT{b}", [FC, 2 * P], F32) for b in range(2)]
    ssilu = sb("ssilu", [P, SF], F32)
    shid = sb("shid", [P, SF], F32)
    shidT = sb("shidT", [FC, SFC * P], F32)
    back = [sb(f"back{r}", [P, D], F32) for r in range(GRING)]
    acc = sb("acc", [P, QT, D], F32)
    stats = sb("stats3", [P, QT, 6], F32)
    mv = sb("mv3", [P, QT, 2], F32)
    var = sb("var3", [P, QT], F32)
    std = sb("std3", [P, QT], F32)
    rstd = sb("rstd3", [P, QT], F32)
    A = [pb(f"A{b}", [P, HALF]) for b in range(2)]
    G = [pb(f"G{b}", [P, HALF]) for b in range(2)]
    H = [pb(f"H{b}", [P, HALF]) for b in range(2)]
    Y = [pb(f"Y{b}", [P, HALF]) for b in range(2)]
    ys = nc.dram_tensor("ys", [TILES * P, D], F32, kind="Internal").ap()

    s_ld = sem("m_ld")
    s_c = sem("m_c")
    s_po = sem("m_po")
    s_ch = sem("m_ch")
    s_tr = sem("m_tr")
    s_x2T = sem("m_x2T")
    s_lg = sem("m_lg")
    s_sub = sem("m_sub")
    s_ex = sem("m_ex")
    s_any = sem("m_any")
    s_rank = sem("m_rank")
    s_ct = sem("m_ct")
    s_ce = sem("m_ce")
    s_past = sem("m_past")
    s_ow = sem("m_ow")
    s_row = sem("m_row")
    s_slot = sem("m_slot")
    s_sc = sem("m_sc")
    s_sg = sem("m_sg")
    s_ss = sem("m_ss")
    s_sh = sem("m_sh")
    s_st = sem("m_st")
    s_shT = sem("m_shT")
    s_sy = sem("m_sy")
    s_acc = sem("m_acc")
    s_xg = [sem(f"m_xg{r}") for r in range(UNROLL)]
    s_w = [sem(f"m_w{r}") for r in range(UNROLL)]
    s_tx = sem("m_tx")
    s_xT = sem("m_xT")
    s_gu = sem("m_gu")
    s_si = sem("m_si")
    s_h = sem("m_h")
    s_th = sem("m_th")
    s_hT = sem("m_hT")
    s_dn = sem("m_dn")
    s_yc = sem("m_yc")
    s_sto = [sem(f"m_sto{r}") for r in range(UNROLL)]
    s_bk = [sem(f"m_bk{r}") for r in range(GRING)]
    s_var, s_std, s_y, s_out = sem("m_var"), sem("m_std"), sem("m_y"), sem("m_out")

    block = ctx.enter_context(nc.Block())
    ROUNDS = TILES // UNROLL

    def steps(engine, step):
        for r in range(UNROLL):
            step(r, r, False)
        with engine.Fori(1, ROUNDS - 1) as i:
            for r in range(UNROLL):
                step(UNROLL * i + r, r, False)
        for r in range(UNROLL):
            step(UNROLL * (ROUNDS - 1) + r, r, True)

    def round_of(n, r):
        return n // UNROLL + 1 if isinstance(n, int) else (n - r) // UNROLL + 1

    def after(engine, s, value, n, first):
        if not (isinstance(n, int) and n < first):
            engine.wait_ge(s, value)

    @block.sync
    def _(sp):
        sp.dma_start(gateT[:, :, :], a["gateT"]).then_inc(s_ld, 16)
        sp.dma_start(swgu[:, :, :], a["swgu"]).then_inc(s_ld, 16)
        sp.dma_start(swd[:, :, :], a["swd"]).then_inc(s_ld, 16)
        sp.wait_ge(s_row, 1)

        def load_weights(n, r):
            e = sp.value_load(owner[0:1, bass.ds(n, 1)], min_val=0, max_val=NE - 1)
            sp.dma_start(wgu[r][:, :], a["wgu"][bass.ds(e, 1), :, :].rearrange("o p n -> p (o n)")).then_inc(s_w[r], 16)
            sp.dma_start(wd[r][:, :], a["wd"][bass.ds(e, 1), :, :].rearrange("o p n -> p (o n)")).then_inc(s_w[r], 16)

        def load_rows(n, r):
            sp.dma_start(xg[r][:, :], xs[bass.ds(n * P, P), :]).then_inc(s_xg[r], 16)

        for r in range(UNROLL):
            load_weights(r, r)
        sp.wait_ge(s_sc, 16 * PICKS)
        for r in range(UNROLL):
            load_rows(r, r)

        def step(n, r, last):
            if not last:
                sp.wait_ge(s_dn, n + 1)
                load_weights(n + UNROLL, r)
                load_rows(n + UNROLL, r)
            sp.wait_ge(s_yc, n + 1)
            sp.dma_start(ys[bass.ds(n * P, P), :], yt[r][:, :]).then_inc(s_sto[r], 16)

        steps(sp, step)
        sp.wait_ge(s_y, QT)
        sp.dma_start(out, acc[:, :, :]).then_inc(s_out, 16)
        sp.wait_ge(s_out, 16)

    @block.gpsimd
    def _(pool):
        order = [0]

        def link(ins):
            order[0] += 1
            ins.then_inc(s_po, 1)
            pool.wait_ge(s_po, order[0])

        def triangle(m, compare, value):
            link(nc.gpsimd.affine_select(out=m, in_=m, compare_op=compare, fill=value, base=0,
                                         pattern=[[-1, m.shape[1]]], channel_multiplier=1))

        link(nc.gpsimd.memset(ident[:, :], 0.0))
        triangle(ident[:, :], ALU.not_equal, 1.0)
        link(nc.gpsimd.iota(iota[:, :], [[1, P]], base=0, channel_multiplier=0, allow_small_or_imprecise_dtypes=True))
        link(nc.gpsimd.memset(before[:, :], 0.0))
        triangle(before[:, :], ALU.is_ge, 1.0)
        link(nc.gpsimd.memset(upto[:, :], 0.0))
        triangle(upto[:, :], ALU.is_gt, 1.0)
        link(nc.gpsimd.memset(onesb[:, :], 1.0))
        link(nc.gpsimd.memset(onesf[:, :], 1.0))
        pool.sem_inc(s_c, 1)

        pool.wait_ge(s_slot, 1)
        for n in range(PICKS):
            nc.gpsimd.indirect_dma_start(xs, bass.IndirectOffsetOnAxis(ap=slots[:, n:n + 1], axis=0), x2[:, n % QT, :],
                                         None).then_inc(s_sc, 16)
        for r in range(UNROLL):
            pool.wait_ge(s_sto[r], 16 * ROUNDS)
        for n in range(PICKS):
            if n >= GRING:
                pool.wait_ge(s_acc, QT + n - GRING + 1)
            nc.gpsimd.indirect_dma_start(back[n % GRING][:, :], None, ys,
                                         bass.IndirectOffsetOnAxis(ap=slots[:, n:n + 1], axis=0)).then_inc(s_bk[n % GRING], 16)

    @block.scalar
    def _(act):
        for qt in range(QT):
            act.wait_ge(s_tr, qt + 1)
            nc.scalar.activation(x2T[:, :, qt * P:(qt + 1) * P], A[qt % 2][:, 0:D]
                                 .rearrange("p (c n) -> p c n", c=DC), ACT.Copy).then_inc(s_x2T, 1)
        act.wait_ge(s_sub, 1)
        nc.scalar.activation(scores[:, :, :], logits[:, :, :], ACT.Exp).then_inc(s_ex, 1)
        for qt in range(QT):
            act.wait_ge(s_sg, 2 * qt + 1)
            if qt >= 1:
                act.wait_ge(s_sh, qt)
            nc.scalar.activation(ssilu[:, :], G[0][:, 0:SF], ACT.Silu).then_inc(s_ss, 1)
            act.wait_ge(s_st, qt + 1)
            if qt >= 1:
                act.wait_ge(s_sy, qt)
            nc.scalar.activation(shidT[:, :], H[0][0:FC, :], ACT.Copy).then_inc(s_shT, 1)

        def move(n, b):
            act.wait_ge(s_tx, n + 1)
            after(act, s_gu, n - 1, n, 2)
            nc.scalar.activation(xgT[b][:, :], A[b][:, 0:D], ACT.Copy).then_inc(s_xT, 1)

        def gate(n, b):
            act.wait_ge(s_gu, n + 1)
            after(act, s_h, n - 1, n, 2)
            nc.scalar.activation(silu[b][:, :], G[b][:, 0:FFN], ACT.Silu).then_inc(s_si, 1)

        move(0, 0)
        move(1, 1)
        gate(0, 0)

        def step(n, r, last):
            if not (last and r == UNROLL - 1):
                gate(n + 1, (r + 1) % 2)
            if not (last and r >= UNROLL - 2):
                move(n + 2, r % 2)

        steps(act, step)
        act.wait_ge(s_var, 1)
        nc.scalar.activation(std[:, :], var[:, :], ACT.Sqrt).then_inc(s_std, 1)

    @block.vector
    def _(dve):
        order = [0]

        def link(ins):
            order[0] += 1
            ins.then_inc(s_ch, 1)
            dve.wait_ge(s_ch, order[0])

        spread = lambda v: v.rearrange("p (q o) -> p q o", o=1).broadcast_to([P, QT, NE])
        dve.wait_ge(s_c, 1)
        dve.wait_ge(s_lg, 1)
        lg = Y[0][:, :].rearrange("p (q e) -> p q e", e=NE)
        link(nc.vector.tensor_reduce(red[:, 0, :], lg, AX.X, ALU.max))
        nc.vector.tensor_tensor(logits[:, :, :], lg, spread(red[:, 0, :]), ALU.subtract).then_inc(s_sub, 1)
        dve.wait_ge(s_ex, 1)
        link(nc.vector.tensor_reduce(red[:, 1, :], scores[:, :, :], AX.X, ALU.add))
        link(nc.vector.reciprocal(red[:, 2, :], red[:, 1, :]))
        link(nc.vector.tensor_tensor(scores[:, :, :], scores[:, :, :], spread(red[:, 2, :]), ALU.mult))
        for qt in range(QT):
            link(nc.vector.max(top[:, qt, :], scores[:, qt, :]))
            link(nc.vector.max_index(topi[:, qt, :], top[:, qt, :], scores[:, qt, :]))
        link(nc.vector.tensor_copy(topf[:, :, :], topi[:, :, :]))
        experts = iota[:, 0:NE].rearrange("p (o e) -> p o e", o=1).broadcast_to([P, QT, NE])
        for j in range(TOPK):
            link(nc.vector.tensor_tensor(chosen[:, j, :, :], experts, spread(topf[:, :, j]), ALU.is_equal))
        nc.vector.tensor_reduce(anyj[:, :, :], chosen[:, :, :, :].rearrange("p j q e -> p (q e) j"), AX.X,
                                ALU.max).then_inc(s_any, 1)
        link(nc.vector.tensor_reduce(red[:, 0, :], top[:, :, 0:TOPK], AX.X, ALU.add))
        link(nc.vector.tensor_scalar(red[:, 1, :], red[:, 0, :], 1e-20, None, ALU.add))
        link(nc.vector.reciprocal(red[:, 3, :], red[:, 1, :]))
        link(nc.vector.tensor_tensor(wt[:, :, :], top[:, :, 0:TOPK].rearrange("p q j -> p j q"),
                                     red[:, 3, :].rearrange("p (o q) -> p o q", o=1).broadcast_to([P, TOPK, QT]),
                                     ALU.mult))
        dve.wait_ge(s_rank, 1)
        link(nc.vector.tensor_scalar(cfill[:, :], H[0][0:NE, 0:1], float(P - 1), None, ALU.add))
        link(nc.vector.tensor_scalar(ctile[:, :], cfill[:, :], 7, None, ALU.logical_shift_right))
        nc.vector.tensor_copy(ctilef[:, :], ctile[:, :]).then_inc(s_ct, 1)
        link(nc.vector.tensor_scalar(filled[:, :], G[1][:, 0:NE], float(P - 1), None, ALU.add))
        link(nc.vector.tensor_scalar(tilesi[:, :], filled[:, :], 7, None, ALU.logical_shift_right))
        link(nc.vector.tensor_copy(tiles[:, :], tilesi[:, :]))
        link(nc.vector.tensor_tensor_scan(ends[:, :], onesf[:, :], tiles[:, :], 0.0, ALU.mult, ALU.add))
        link(nc.vector.tensor_tensor(base[:, :], ends[:, :], tiles[:, :], ALU.subtract))
        link(nc.vector.tensor_scalar(base[:, :], base[:, :], float(P), None, ALU.mult))
        link(nc.vector.tensor_tensor(where[:, :, :], Y[1][:, :].rearrange("p (q e) -> p q e", e=NE),
                                     base[:, :].rearrange("p (o e) -> p o e", o=1).broadcast_to([P, QT, NE]), ALU.add))
        for j in range(TOPK):
            link(nc.vector.tensor_tensor(place[:, j, :, :], chosen[:, j, :, :], where[:, :, :], ALU.mult))
        link(nc.vector.tensor_reduce(slotf[:, :], place[:, :, :, :].rearrange("p j q e -> p (j q) e"), AX.X, ALU.add))
        nc.vector.tensor_copy(slots[:, :], slotf[:, :]).then_inc(s_slot, 1)
        dve.wait_ge(s_ce, 1)
        link(nc.vector.tensor_copy(cend[:, :], H[0][0:NE, 1:2]))
        nc.vector.tensor_scalar(past[:, :], iota[0:NE, 0:TILES], cend[:, 0:1], None, ALU.is_ge).then_inc(s_past, 1)
        dve.wait_ge(s_ow, 1)
        nc.vector.tensor_scalar(owner[:, :], H[0][0:1, P:P + TILES], float(NE - 1), None, ALU.min).then_inc(s_row, 1)
        for qt in range(QT):
            dve.wait_ge(s_ss, qt + 1)
            dve.wait_ge(s_sg, 2 * qt + 2)
            if qt >= 1:
                dve.wait_ge(s_st, qt)
            nc.vector.tensor_tensor(shid[:, :], G[1][:, 0:SF], ssilu[:, :], ALU.mult).then_inc(s_sh, 1)
            dve.wait_ge(s_sy, qt + 1)
            nc.vector.tensor_tensor(acc[:, qt, :], Y[0][:, 0:D], x2[:, qt, :], ALU.add).then_inc(s_acc, 1)

        def multiply(n, b):
            dve.wait_ge(s_si, n + 1)
            after(dve, s_th, n - 1, n, 2)
            nc.vector.tensor_tensor(hid[b][:, :], G[b][:, FFN:2 * FFN], silu[b][:, :], ALU.mult).then_inc(s_h, 1)

        multiply(0, 0)

        def step(n, r, last):
            b = r % 2
            dve.wait_ge(s_th, n + 1)
            after(dve, s_dn, n - 1, n, 2)
            nc.vector.tensor_copy(hidT[b][:, :], H[b][0:FC, 0:2 * P]).then_inc(s_hT, 1)
            if not (last and r == UNROLL - 1):
                multiply(n + 1, (r + 1) % 2)
            dve.wait_ge(s_dn, n + 1)
            after(dve, s_sto[r], 16 * (round_of(n, r) - 1), n, UNROLL)
            nc.vector.tensor_copy(yt[r][:, :], Y[b][:, 0:D]).then_inc(s_yc, 1)

        steps(dve, step)
        for n in range(PICKS):
            j, qt = n // QT, n % QT
            dve.wait_ge(s_bk[n % GRING], 16 * (n // GRING + 1))
            dve.wait_ge(s_acc, n + 1)
            nc.vector.scalar_tensor_tensor(out=acc[:, qt, :], in0=back[n % GRING][:, :], scalar=wt[:, j, qt:qt + 1],
                                           in1=acc[:, qt, :], op0=ALU.mult, op1=ALU.add).then_inc(s_acc, 1)
        dve.wait_ge(s_acc, QT + PICKS)
        for qt in range(QT):
            link(nc.vector.bn_stats(stats[:, qt, :], acc[:, qt, :]))
            link(nc.vector.bn_aggr(mv[:, qt, :], stats[:, qt, :]))
        nc.vector.tensor_scalar(var[:, :], mv[:, :, 1], EPS, None, ALU.add).then_inc(s_var, 1)
        dve.wait_ge(s_std, 1)
        link(nc.vector.reciprocal(rstd[:, :], std[:, :]))
        for qt in range(QT):
            nc.vector.tensor_scalar(acc[:, qt, :], acc[:, qt, :], mv[:, qt, 0:1], rstd[:, qt:qt + 1], ALU.subtract,
                                    ALU.mult).then_inc(s_y, 1)

    @block.tensor
    def _(pe):
        pe.wait_ge(s_c, 1)
        for qt in range(QT):
            if qt >= 2:
                pe.wait_ge(s_x2T, qt - 1)
            for c in range(DC):
                last = nc.tensor.transpose(A[qt % 2][:, c * P:(c + 1) * P], x2[:, qt, c * P:(c + 1) * P], ident[:, :])
            last.then_inc(s_tr, 1)
        pe.wait_ge(s_x2T, QT)
        pe.wait_ge(s_ld, 48)
        for qt in range(QT):
            for c in range(DC):
                last = nc.tensor.matmul(Y[0][:, qt * NE:(qt + 1) * NE], x2T[:, c, qt * P:(qt + 1) * P],
                                        gateT[:, c, :], start=(c == 0), stop=(c == DC - 1))
        last.then_inc(s_lg, 1)
        pe.wait_ge(s_any, 1)
        for qt in range(QT):
            for s in range(qt + 1):
                nc.tensor.matmul(Y[1][:, qt * NE:(qt + 1) * NE], (before if s == qt else onesb)[:, :], anyj[:, s, :],
                                 start=(s == 0), stop=(s == qt))
        for s in range(QT):
            nc.tensor.matmul(G[1][:, 0:NE], onesb[:, :], anyj[:, s, :], start=(s == 0), stop=(s == QT - 1))
        for s in range(QT):
            last = nc.tensor.matmul(H[0][0:NE, 0:1], anyj[:, s, :], onesb[:, 0:1], start=(s == 0), stop=(s == QT - 1))
        last.then_inc(s_rank, 1)
        pe.wait_ge(s_ct, 1)
        nc.tensor.matmul(H[0][0:NE, 1:2], upto[:, :], ctilef[:, :], start=True, stop=True).then_inc(s_ce, 1)
        pe.wait_ge(s_past, 1)
        nc.tensor.matmul(H[0][0:1, P:P + TILES], onesf[0:NE, 0:1], past[:, :], start=True, stop=True).then_inc(s_ow, 1)
        pe.wait_ge(s_row, 1)
        for qt in range(QT):
            if qt >= 1:
                pe.wait_ge(s_sh, qt)
            for w in range(2):
                for c in range(DC):
                    last = nc.tensor.matmul(G[w][:, 0:SF], x2T[:, c, qt * P:(qt + 1) * P], swgu[:, c, w * SF:(w + 1) * SF],
                                            start=(c == 0), stop=(c == DC - 1))
                last.then_inc(s_sg, 1)
            pe.wait_ge(s_sh, qt + 1)
            if qt >= 1:
                pe.wait_ge(s_shT, qt)
            for f in range(SFC):
                last = nc.tensor.transpose(H[0][0:FC, f * P:(f + 1) * P], shid[:, f * FC:(f + 1) * FC], ident[:, :])
            last.then_inc(s_st, 1)
            pe.wait_ge(s_shT, qt + 1)
            if qt >= 1:
                pe.wait_ge(s_acc, qt)
            for f in range(SFC):
                last = nc.tensor.matmul(Y[0][:, 0:D], shidT[:, f * P:(f + 1) * P], swd[:, f, :],
                                        start=(f == 0), stop=(f == SFC - 1))
            last.then_inc(s_sy, 1)
        pe.wait_ge(s_acc, QT)

        def turn_rows(n, r, b):
            pe.wait_ge(s_xg[r], 16 * round_of(n, r))
            after(pe, s_xT, n - 1, n, 2)
            for c in range(DC):
                last = nc.tensor.transpose(A[b][:, c * P:(c + 1) * P], xg[r][:, c * P:(c + 1) * P], ident[:, :])
            last.then_inc(s_tx, 1)

        def gate_up(n, r, b):
            pe.wait_ge(s_w[r], 32 * round_of(n, r))
            pe.wait_ge(s_xT, n + 1)
            after(pe, s_h, n - 1, n, 2)
            for c in range(DC):
                last = nc.tensor.matmul(G[b][:, 0:2 * FFN], xgT[b][:, c * P:(c + 1) * P],
                                        wgu[r][:, c * 2 * FFN:(c + 1) * 2 * FFN], start=(c == 0), stop=(c == DC - 1))
            last.then_inc(s_gu, 1)

        turn_rows(0, 0, 0)
        turn_rows(1, 1, 1)
        gate_up(0, 0, 0)

        def step(n, r, last_round):
            b = r % 2
            pe.wait_ge(s_h, n + 1)
            after(pe, s_hT, n - 1, n, 2)
            for f in range(2):
                last = nc.tensor.transpose(H[b][0:FC, f * P:(f + 1) * P], hid[b][:, f * FC:(f + 1) * FC], ident[:, :])
            last.then_inc(s_th, 1)
            if not (last_round and r == UNROLL - 1):
                gate_up(n + 1, (r + 1) % UNROLL, (r + 1) % 2)
            pe.wait_ge(s_hT, n + 1)
            after(pe, s_yc, n - 1, n, 2)
            for f in range(2):
                last = nc.tensor.matmul(Y[b][:, 0:D], hidT[b][:, f * P:(f + 1) * P], wd[r][:, f * D:(f + 1) * D],
                                        start=(f == 0), stop=(f == 1))
            last.then_inc(s_dn, 1)
            if not (last_round and r >= UNROLL - 2):
                turn_rows(n + 2, (r + 2) % UNROLL, b)

        steps(pe, step)


def program(nc, a, out):
    xs = nc.dram_tensor("xs", [TILES * P, D], F32, kind="Internal").ap()
    with nc.sbuf_tensor("x2", [P, QT, D], F32) as x2:
        with nc.sbuf_tensor("oT", [P, HEADS, T], F32) as oT:
            with ExitStack() as ctx:
                attention(nc, ctx, a, oT, xs)
            with ExitStack() as ctx:
                project_and_experts(nc, ctx, a, oT, x2)
        with ExitStack() as ctx:
            mixture(nc, ctx, a, x2, out, xs)


def kernel(x, itok_BxS_13_99985, ctx_2048, L0_attn_kv_k, L0_attn_kv_v, L0_attn_Wq, L0_attn_Wo, L0_ffn_gate_w,
           L0_ffn_w_gate_up, L0_ffn_w_down, L0_ffn_ws_gate_up, L0_ffn_ws_down):
    import concourse.bacc as bacc
    from concourse.bass_utils import run_bass_kernel_spmd as run

    chunks = lambda m: np.ascontiguousarray(m.reshape(-1, P, m.shape[1]).transpose(1, 0, 2))
    xs = np.asarray(x).reshape(T, D)
    wo = np.asarray(L0_attn_Wo).T.reshape(4, 4, HD, D)
    wo_pad = np.zeros((4, 4, 32, D), wo.dtype)
    wo_pad[:, :, :HD] = wo
    arrays = {
        "x": chunks(xs),
        "xT": chunks(xs.T),
        "wqT": chunks(np.asarray(L0_attn_Wq).T),
        "woT": chunks(wo_pad.reshape(4 * P, D)),
        "kT": chunks(np.asarray(L0_attn_kv_k).reshape(KV, D).T),
        "v": np.ascontiguousarray(np.asarray(L0_attn_kv_v).reshape(KT, P, HEADS, HD).transpose(2, 1, 0, 3)
                                  .reshape(HEADS, P, KT * HD)),
        "ids": np.ascontiguousarray(np.asarray(itok_BxS_13_99985).reshape(T)),
        "ctxT": np.ascontiguousarray(np.asarray(ctx_2048).transpose(0, 2, 1).reshape(E1, DC, P, F1)
                                     .transpose(2, 0, 1, 3)),
    }
    rows = lambda m, p: np.ascontiguousarray(m.transpose(0, 2, 1).reshape(m.shape[0], -1, p, m.shape[1])
                                             .transpose(0, 2, 1, 3))
    arrays["wgu"] = rows(np.asarray(L0_ffn_w_gate_up), P).reshape(NE, P, DC * 2 * FFN)
    arrays["wd"] = rows(np.asarray(L0_ffn_w_down), FC).reshape(NE, FC, 2 * D)
    arrays["swgu"] = rows(np.asarray(L0_ffn_ws_gate_up)[None], P)[0]
    arrays["swd"] = rows(np.asarray(L0_ffn_ws_down)[None], FC)[0]
    arrays["gateT"] = chunks(np.asarray(L0_ffn_gate_w).T)
    nc = bacc.Bacc("TRN2", target_bir_lowering=False, num_devices=1)
    a = {n: nc.dram_tensor(n + "_in", v.shape, mybir.dt.from_np(v.dtype), kind="ExternalInput").ap()
         for n, v in arrays.items()}
    out = nc.dram_tensor("out", (P, QT, D), F32, kind="ExternalOutput").ap()
    program(nc, a, out)
    r = run(nc, [{n + "_in": v for n, v in arrays.items()}], core_ids=[0])
    return np.ascontiguousarray(r.results[0]["out"].transpose(1, 0, 2)).reshape(4, 256, D)
```

```python
import numpy as np
import concourse.bass as bass
from concourse import mybir
from contextlib import ExitStack

F32 = mybir.dt.float32
BF16 = mybir.dt.bfloat16
I32 = mybir.dt.int32
U32 = mybir.dt.uint32
ALU = mybir.AluOpType
ACT = mybir.ActivationFunctionType
AX = mybir.AxisListType

P = 128
T, D = 1024, 256
DC = D // P
QT = T // P
HEADS, HD = 16, 16
KV = 4096
KT = KV // P
SCALE = 1.0 / 4.0
EPS = 1e-5

GROUPS = [(0, 0), (0, 1), (0, 2), (1, 0), (1, 1), (2, 0)]
RUNS = [(0, 3), (1, 2), (2, 1)]
ROWS = len(GROUPS) * HD
MROWS = 3
RING = 4
AHEAD = 3
HALF = 512
PAIRS = QT * KV // 1024
FIRST_PAIRS = 5
STEPS = 2 * KT
ROWS_AT = (STEPS - 4, STEPS - 1)
STARTED = 3
SLOTS = 4
SG = STEPS // 4
CHS = [1024, 512]

E1 = 4
F1 = 256
VOCAB = 12500


def attention(nc, ctx, a, oT, keep):
    sb = lambda name, shape, dt: ctx.enter_context(nc.sbuf_tensor(name, shape, dt))
    pb = lambda name, shape: ctx.enter_context(nc.psum_tensor(name, shape, F32))
    sem = lambda name: ctx.enter_context(nc.semaphore(name))

    flat = oT[:, :, :].rearrange("p h t -> p (h t)")
    taken = [0]

    def early(*shape):
        size = int(np.prod(shape))
        view = flat[:, taken[0]:taken[0] + size]
        taken[0] += size
        if len(shape) > 1:
            view = view.rearrange("p (a n) -> p a n", a=shape[0])
        return view

    def early_bf16(*shape):
        size = int(np.prod(shape))
        view = flat[:, taken[0]:taken[0] + size // 2].bitcast(BF16)
        taken[0] += size // 2
        names = {2: ("p (a n) -> p a n", {"a": shape[0]}),
                 3: ("p (a b n) -> p a b n", {"a": shape[0], "b": shape[1] if len(shape) > 2 else 1})}
        return view.rearrange(names[len(shape)][0], **names[len(shape)][1])

    xT = early(DC, T)
    wqT = early(DC, D)
    kstack = [sb(f"kstack{b}", [ROWS + MROWS, KV], BF16) for b in range(RING)]
    qstack = [sb(f"qstack{b}", [ROWS + MROWS, T], BF16) for b in range(RING)]
    ksrc = [[early(CHS[0]) for i in range(4)], [sb(f"ksrc{i}", [P, CHS[1]], F32) for i in range(2)]]
    kres = [[early(CHS[0]) for i in range(2)], [sb(f"kres{i}", [P, CHS[1]], F32) for i in range(2)]]
    kpart = [[early_bf16(3, CHS[0]) for i in range(3)], [sb(f"kpart{i}", [P, 3, CHS[1]], BF16) for i in range(2)]]
    qpart = early_bf16(4, 3, HALF)
    vstage = [sb(f"vstage{b}", [P, KT, HD], F32) for b in range(2)]
    vpad = [sb(f"vpad{b}", [P, KT, 32], F32) for b in range(2)]
    weights = sb("weights", [P, SLOTS, 4, HALF], F32)
    wflat = weights[:, :, :, :].rearrange("p a b n -> p (a b n)")
    keep = dict(keep, ids=wflat[:, 0:T].bitcast(I32), idf=wflat[:, T:2 * T],
                ge=wflat[:, 2 * T:5 * T].rearrange("p (e t) -> p e t", e=3))
    mx4 = sb("mx4", [P, QT, 4], F32)
    mres = sb("mres", [P, QT], F32)
    mres2 = sb("mres2", [P, QT], F32)
    m3 = sb("m3", [P, QT, 3], BF16)
    ident = sb("ident_bf", [P, P], BF16)
    zero = sb("zero", [P, KT * HD], F32)

    Mb = pb("Mb", [P, 2, 1024])
    Sb = pb("Sb", [P, 3, HALF])
    Ob = pb("Ob", [P, HALF])
    Qb = [Mb[:, 0, 0:HALF], Mb[:, 1, 0:HALF], Sb[:, 0, :], Sb[:, 1, :]]

    kparts = nc.dram_tensor("kparts", [3, D, KV], BF16, kind="Internal").ap()
    qparts = nc.dram_tensor("qparts", [3, D, T], BF16, kind="Internal").ap()

    s_x = sem("s_x")
    s_ksrc = [[sem(f"s_ksrc{c}{i}") for i in range(len(ksrc[c]))] for c in range(DC)]
    s_q = sem("s_q")
    s_hm = sem("s_hm")
    s_rl = sem("s_rl")
    s_kp = sem("s_kp")
    s_kpo = sem("s_kpo")
    s_qw = sem("s_qw")
    s_kw = [[sem(f"s_kw{c}{i}") for i in range((4, 2)[c])] for c in range(DC)]
    s_qfirst = sem("s_qfirst")
    s_first = [sem(f"s_first{i}") for i in range(4)]
    s_zero = sem("s_zero")
    s_const = sem("s_const")
    s_stack = [sem(f"s_stack{b}") for b in range(RING)]
    s_vload = [sem(f"s_vload{b}") for b in range(2)]
    s_v = sem("s_v")
    s_mx = sem("s_mx")
    s_mred = sem("s_mred")
    s_mch = sem("s_mch")
    s_mid = sem("s_mid")
    s_m3 = sem("s_m3")
    s_mt = sem("s_mt")
    s_qm = sem("s_qm")
    s_st = sem("s_st")
    s_exp = sem("s_exp")
    s_pv = sem("s_pv")
    s_ot = sem("s_ot")
    s_ids = sem("s_ids")

    block = ctx.enter_context(nc.Block())
    LOADED = 2 * len(RUNS) * 16
    NCHS = [KV // ch for ch in CHS]

    UNITS = [("k", 0), ("k", 1), ("q", 0), ("q", 1)] + [("k", i) for i in range(2, NCHS[0])] + [("q", 2), ("q", 3)]

    def unit(u):
        kind, i = UNITS[u]
        if kind == "q":
            return Qb[i], kres[0][u % 2][:, 0:HALF], [qpart[:, i, part, :] for part in range(3)]
        return ksrc[0][i], kres[0][u % 2], [kpart[0][i % 3][:, part, :] for part in range(3)]

    TURNS = [(0, 0)] + [turn for u in range(len(UNITS)) for turn in ((u + 1, 0), (u, 1)) if turn[0] < len(UNITS)]
    nth_turn = {turn: n + 1 for n, turn in enumerate(TURNS)}

    RING_OF = [(kind, k) for n in range(STEPS)
               for kind, k in [("row", half) for half in range(2) if ROWS_AT[half] == n] + [("block", n)]]

    def bank(kind, k):
        return RING_OF.index((kind, k)) % 3

    LAST_BANKS = [Sb[:, n, :] for n in range(3)] + [Mb[:, n // 2, n % 2 * HALF:(n % 2 + 1) * HALF] for n in range(4)]

    def block_bank(n, last):
        return LAST_BANKS[n % len(LAST_BANKS)] if last else Sb[:, bank("block", n), :]

    def bank_free(h, kind, k):
        at = RING_OF.index((kind, k)) - 3
        kind, k = RING_OF[at]
        before = at < 0
        if kind == "row":
            return s_qm, 2 * (h - before) + 3 + k
        return s_exp, STEPS * (h - before) + k + 1

    @block.sync
    def _(sp):
        def load_chunk(c, i):
            buffers = len(ksrc[c])
            if i >= buffers:
                sp.wait_ge(s_kp, i - buffers + 1)
            sp.dma_start(ksrc[c][i % buffers][:, :], a["kT"][:, c, i * CHS[c]:(i + 1) * CHS[c]]
                         ).then_inc(s_ksrc[c][i % buffers], 16)

        def store_chunk(c, i):
            if c == 0:
                sp.wait_ge(s_rl, nth_turn[UNITS.index(("k", i)), 1])
            else:
                sp.wait_ge(s_kp, i + 1)
            sp.dma_start(kparts[:, c * P:(c + 1) * P, i * CHS[c]:(i + 1) * CHS[c]].rearrange("a p n -> p a n"),
                         kpart[c][i % (3, 2)[c]][:, :, :]).then_inc(s_kw[c][i % (4, 2)[c]], 16)

        def store_q(n):
            sp.wait_ge(s_rl, nth_turn[UNITS.index(("q", n)), 1])
            c, half = n // 2, n % 2
            sp.dma_start(qparts[:, c * P:(c + 1) * P, half * HALF:(half + 1) * HALF].rearrange("a p n -> p a n"),
                         qpart[:, n, :, :]).then_inc(s_qw, 16)

        def first_stack(i):
            sp.wait_ge(s_kw[0][i], 16)
            keys, row = slice(i * CHS[0], (i + 1) * CHS[0]), 0
            for part, n in RUNS:
                sp.dma_start(kstack[0][row:row + n * HD, keys],
                             kparts[part:part + 1, 0:HD, keys].broadcast_to([n, HD, CHS[0]])).then_inc(s_first[i], 16)
                row += n * HD

        def load_stack(h, b):
            row = 0
            for part, n in RUNS:
                rows = slice(row, row + n * HD)
                sp.dma_start(kstack[b][rows, :],
                             kparts[part:part + 1, bass.ds(h * HD, HD), :].broadcast_to([n, HD, KV])
                             ).then_inc(s_stack[b], 16)
                sp.dma_start(qstack[b][rows, :],
                             qparts[0:n, bass.ds(h * HD, HD), :]).then_inc(s_stack[b], 16)
                row += n * HD

        def load_v(h, b):
            sp.dma_start(vstage[b][:, :, :], a["v"][bass.ds(h, 1), :, :].rearrange("o p n -> p (o n)")
                         .rearrange("p (k d) -> p k d", k=KT)).then_inc(s_vload[b], 16)

        sp.dma_start(wqT[:, :, :], a["wqT"]).then_inc(s_x, 16)
        load_chunk(0, 0)
        sp.dma_start(xT[:, :, :], a["xT"]).then_inc(s_x, 16)
        for i in range(1, NCHS[0]):
            load_chunk(0, i)
        sp.dma_start(keep["ids"][:, :], a["ids"].rearrange("(o t) -> o t", o=1).broadcast_to([P, T])).then_inc(s_ids, 16)
        load_v(0, 0)
        load_v(1, 1)
        store_chunk(0, 0)
        store_chunk(0, 1)
        store_q(0)
        store_q(1)
        first_stack(0)
        sp.wait_ge(s_qw, 2 * 16)
        row = 0
        for part, n in RUNS:
            sp.dma_start(qstack[0][row:row + n * HD, :], qparts[0:n, 0:HD, :]).then_inc(s_qfirst, 16)
            row += n * HD
        for i in range(1, NCHS[0]):
            if i + 1 < NCHS[0]:
                store_chunk(0, i + 1)
            first_stack(i)
        for h in range(1, AHEAD):
            load_stack(h, h)
        store_q(2)
        store_q(3)
        for i in range(2):
            load_chunk(1, i)
        for i in range(NCHS[1]):
            if i + 2 < NCHS[1]:
                load_chunk(1, i + 2)
            store_chunk(1, i)
        for i in range(2):
            sp.wait_ge(s_kw[1][i], 16 * (NCHS[1] // 2))

        def head(h, b, stack, v):
            if v:
                sp.wait_ge(s_v, h)
                load_v(h + 1, (b + 1) % 2)
            if stack:
                sp.wait_ge(s_st, h * STEPS)
                load_stack(h + AHEAD, (b + AHEAD) % RING)

        sp.wait_ge(s_qw, 4 * 16)
        load_stack(AHEAD, AHEAD)
        for name in ("x", "woT", "ctxT", "gateT", "swgu", "swd"):
            sp.dma_start(keep[name], a[name]).then_inc(keep["s_ld"], 16)
        for h in range(1, RING):
            head(h, h, True, True)
        with sp.Fori(1, HEADS // RING - 1) as i:
            for b in range(RING):
                head(RING * i + b, b, True, True)
        for h in range(HEADS - RING, HEADS):
            head(h, h % RING, h + AHEAD < HEADS, h + 1 < HEADS)
        sp.wait_ge(keep["s_ld"], 6 * 16)

    @block.gpsimd
    def _(pool):
        order = [0]

        def link(ins):
            order[0] += 1
            ins.then_inc(s_kpo, 1)
            pool.wait_ge(s_kpo, order[0])

        def select(m, compare, base=0, pattern=None, fill=1.0):
            link(nc.gpsimd.affine_select(out=m, in_=m, compare_op=compare, fill=fill, base=base,
                                         pattern=pattern or [[-1, m.shape[1]]], channel_multiplier=1))

        for m in (ident[:, :], keep["ident"], keep["pick"], keep["spread"], keep["before"], keep["upto"]):
            link(nc.gpsimd.memset(m, 0.0))
        select(ident[:, :], ALU.not_equal)
        select(keep["ident"], ALU.not_equal)
        for j in range(2):
            for g in range(4):
                select(keep["pick"][:, j, j * HD:(j + 1) * HD], ALU.not_equal, base=-32 * g)
        for part in range(3):
            select(keep["spread"], ALU.not_equal, base=-HEADS * part, pattern=[[-1, HEADS], [0, HD]])
        select(keep["before"], ALU.is_ge)
        select(keep["upto"], ALU.is_gt)
        link(nc.gpsimd.memset(keep["onesb"], 1.0))
        link(nc.gpsimd.memset(keep["onesf"], 1.0))
        link(nc.gpsimd.iota(keep["iota"], [[1, P]], base=0, channel_multiplier=0, allow_small_or_imprecise_dtypes=True))
        for b in range(2):
            link(nc.gpsimd.memset(vpad[b][:, :, HD:32], 0.0))
            link(nc.gpsimd.memset(vpad[b][:, :, HD:HD + 1], 1.0))
        pool.wait_ge(s_zero, 1)

        def pad_v(h, b, nth, waits):
            pool.wait_ge(s_vload[b], 16 * nth)
            if waits:
                pool.wait_ge(s_pv, SLOTS + (h - 1) * SG)
                pool.wait_ge(s_v, h)
            nc.gpsimd.tensor_tensor(vpad[b][:, :, 0:HD], vstage[b][:, :, :],
                                    zero[:, :].rearrange("p (k d) -> p k d", k=KT), ALU.add).then_inc(s_v, 1)

        pad_v(0, 0, 1, False)
        pool.wait_ge(s_v, 1)
        pool.wait_ge(s_ids, 16)
        link(nc.gpsimd.tensor_copy(keep["idf"], keep["ids"]))
        for e in range(3):
            link(nc.gpsimd.tensor_scalar(keep["ge"][:, e, :], keep["idf"], float((e + 1) * (VOCAB // E1)), None,
                                         ALU.is_ge))
        link(nc.gpsimd.tensor_scalar(keep["mask"][:, 0, :], keep["ge"][:, 0, :], -1.0, 1.0, ALU.mult, ALU.add))
        for e in range(1, 3):
            link(nc.gpsimd.tensor_tensor(keep["mask"][:, e, :], keep["ge"][:, e - 1, :], keep["ge"][:, e, :],
                                         ALU.subtract))
        link(nc.gpsimd.tensor_copy(keep["mask"][:, 3, :], keep["ge"][:, 2, :]))
        for b in range(RING):
            link(nc.gpsimd.memset(kstack[b][ROWS:ROWS + MROWS, :], -1.0))
        pool.sem_inc(s_const, 1)
        pad_v(1, 1, 1, False)
        pool.wait_ge(s_v, 2)
        for i in range(NCHS[1]):
            pool.wait_ge(s_ksrc[1][i % 2], 16 * (i // 2 + 1))
            if i >= 2:
                pool.wait_ge(s_kw[1][i % 2], 16 * (i // 2))
            src, res, part = ksrc[1][i % 2], kres[1][i % 2], kpart[1][i % 2]
            link(nc.gpsimd.tensor_copy(part[:, 0, :], src[:, :]))
            link(nc.gpsimd.tensor_tensor(res[:, :], src[:, :], part[:, 0, :], ALU.subtract))
            link(nc.gpsimd.tensor_copy(part[:, 1, :], res[:, :]))
            nc.gpsimd.tensor_tensor(part[:, 2, :], res[:, :], part[:, 1, :], ALU.subtract).then_inc(s_kp, 1)
            pool.wait_ge(s_kp, i + 1)
        for h in range(2, RING):
            pad_v(h, h % 2, h // 2 + 1, True)
        with pool.Fori(1, HEADS // RING) as i:
            for b in range(RING):
                pad_v(RING * i + b, b % 2, 2 * i + b // 2 + 1, True)

    @block.scalar
    def _(act):
        for u, second in TURNS:
            (kind, i), (src, res, part) = UNITS[u], unit(u)
            if second:
                act.wait_ge(s_rl, nth_turn[u, 0])
                nc.scalar.activation(part[1], res[:, :], ACT.Copy).then_inc(s_hm, 1)
            else:
                if kind == "q":
                    act.wait_ge(s_q, i + 1)
                else:
                    act.wait_ge(s_ksrc[0][i], 16)
                    if i >= 3:
                        act.wait_ge(s_kw[0][i - 3], 16)
                nc.scalar.activation(part[0], src[:, :], ACT.Copy).then_inc(s_hm, 1)

        def move_rows(h, b, half):
            act.wait_ge(s_mt, 2 * h + half + 1)
            nc.scalar.activation(qstack[b][ROWS:ROWS + MROWS, half * HALF:(half + 1) * HALF],
                                 Sb[ROWS:ROWS + MROWS, bank("row", half), :], ACT.Copy).then_inc(s_qm, 1)

        def exps(h, first, end, last=False):
            for n in range(first, end):
                g = n // 4
                act.wait_ge(s_st, STEPS * h + n + 1)
                if n % 4 == 0:
                    act.wait_ge(s_pv, SLOTS + SG * h + g - (SLOTS - 1))
                nc.scalar.activation(weights[:, g % SLOTS, n % 4, :], block_bank(n, last), ACT.Exp, scale=SCALE
                                     ).then_inc(s_exp, 1)

        def move_sums(h, half):
            act.wait_ge(s_pv, SLOTS + SG * h + (half + 1) * SG // 2)
            nc.scalar.activation(oT[:, bass.ds(h, 1), half * HALF:(half + 1) * HALF].rearrange("p o n -> p (o n)"),
                                 Ob[:, :], ACT.Copy).then_inc(s_ot, 1)

        def head(h, b, last):
            exps(h, STARTED, KT + STARTED, last)
            move_sums(h, 0)
            exps(h, KT + STARTED, ROWS_AT[0], last)
            if not last:
                move_rows(h + 1, (b + 1) % RING, 0)
            exps(h, ROWS_AT[0], ROWS_AT[1], last)
            if not last:
                move_rows(h + 1, (b + 1) % RING, 1)
            exps(h, ROWS_AT[1], STEPS, last)
            if not last:
                exps(h + 1, 0, STARTED)
            move_sums(h, 1)

        for half in range(2):
            move_rows(0, 0, half)
        exps(0, 0, STARTED)
        with act.Fori(0, HEADS // RING - 1) as i:
            for b in range(RING):
                head(RING * i + b, b, False)
        for h in range(HEADS - RING, HEADS):
            head(h, h % RING, h == HEADS - 1)

    @block.vector
    def _(dve):
        nc.vector.memset(zero[:, :], 0.0).then_inc(s_zero, 1)
        for u, second in TURNS:
            src, res, part = unit(u)
            if second:
                dve.wait_ge(s_hm, nth_turn[u, 1])
                dve.wait_ge(s_rl, nth_turn[u, 0])
                nc.vector.tensor_tensor(part[2], res[:, :], part[1], ALU.subtract).then_inc(s_rl, 1)
            else:
                dve.wait_ge(s_hm, nth_turn[u, 0])
                if u >= 2:
                    dve.wait_ge(s_rl, nth_turn[u - 2, 1])
                nc.vector.tensor_tensor(res[:, :], src[:, :], part[0], ALU.subtract).then_inc(s_rl, 1)

        def link(ins, count):
            ins.then_inc(s_mch, 1)
            dve.wait_ge(s_mch, count)

        CHAIN = 3

        def high_part(h, first):
            if not first:
                dve.wait_ge(s_mt, 2 * h)
            dve.wait_ge(s_mred, PAIRS * (h + 1))
            link(nc.vector.tensor_reduce(mres[:, :], mx4[:, :, :], AX.X, ALU.max), CHAIN * h + 1)
            nc.vector.tensor_copy(m3[:, :, 0], mres[:, :]).then_inc(s_mch, 1)

        def middle_part(h):
            dve.wait_ge(s_mch, CHAIN * h + 2)
            link(nc.vector.tensor_tensor(mres2[:, :], mres[:, :], m3[:, :, 0], ALU.subtract), CHAIN * h + 3)
            nc.vector.tensor_copy(m3[:, :, 1], mres2[:, :]).then_inc(s_mid, 1)

        def low_part(h):
            dve.wait_ge(s_mid, h + 1)
            nc.vector.tensor_tensor(m3[:, :, 2], mres2[:, :], m3[:, :, 1], ALU.subtract).then_inc(s_m3, 1)

        def maxima(h, first, chain):
            for j in range(PAIRS):
                qt, kc = (j % QT, j // QT) if first else (j // 4, j % 4)
                dve.wait_ge(s_mx, PAIRS * h + j + 1)
                nc.vector.tensor_reduce(mx4[:, qt, kc:kc + 1], Mb[:, j % 2, :], AX.X, ALU.max).then_inc(s_mred, 1)
                if chain and j == 0:
                    middle_part(h - 1)
                if chain and j == 1:
                    low_part(h - 1)
            high_part(h, first)

        maxima(0, True, False)
        middle_part(0)
        low_part(0)
        maxima(1, False, False)
        with dve.Fori(0, HEADS // RING - 1) as i:
            for b in range(RING):
                maxima(RING * i + b + 2, False, True)
        for h in range(HEADS - RING + 2, HEADS):
            maxima(h, False, True)
        middle_part(HEADS - 1)
        low_part(HEADS - 1)

    @block.tensor
    def _(pe):
        pe.wait_ge(s_x, 32)
        for n in range(4):
            c, half = n // 2, n % 2
            for k in range(DC):
                last = nc.tensor.matmul(Qb[n], wqT[:, k, c * P:(c + 1) * P],
                                        xT[:, k, half * HALF:(half + 1) * HALF], start=(k == 0), stop=(k == DC - 1))
            last.then_inc(s_q, 1)

        def pair(h, b, j, u, first):
            if u == 0 and not (first and j < 2):
                pe.wait_ge(s_mred, PAIRS * h + j - 1)
            qt, kc = (j % QT, j // QT) if first else (j // 4, j % 4)
            if first and u == 0 and qt == 0:
                pe.wait_ge(s_first[kc], len(RUNS) * 16)
            k0 = kc * 1024 + u * HALF
            last = nc.tensor.matmul(Mb[:, j % 2, u * HALF:(u + 1) * HALF], qstack[b][0:ROWS, qt * P:(qt + 1) * P],
                                    kstack[b][0:ROWS, k0:k0 + HALF], start=True, stop=True)
            if u == 1:
                last.then_inc(s_mx, 1)

        def max_rows(h, half):
            for qt in range(4):
                last = nc.tensor.matmul(Sb[ROWS:ROWS + MROWS, bank("row", half), qt * P:(qt + 1) * P], m3[:, 4 * half + qt, :],
                                        ident[:, :], start=True, stop=True)
            last.then_inc(s_mt, 1)

        def weigh(h, b, g):
            half, s = g // (SG // 2), g % (SG // 2)
            if s == 0:
                if g == 0:
                    pe.wait_ge(s_v, h + 1)
                pe.wait_ge(s_ot, 2 * h + half + 1)
            pe.wait_ge(s_exp, STEPS * h + 4 * g + 4)
            for c in range(4):
                last = nc.tensor.matmul(Ob[32 * c:32 * c + 32, :], vpad[b % 2][:, 4 * s + c, :],
                                        weights[:, g % SLOTS, c, :], start=(s == 0), stop=(s == SG // 2 - 1),
                                        skip_group_check=True)
            last.then_inc(s_pv, 1)

        def steps(h, b, nth, left, first, end):
            for n in range(first, end):
                half, kt = n // KT, n % KT
                if n in ROWS_AT and left >= 1:
                    if n == ROWS_AT[0]:
                        pe.wait_ge(s_m3, h + 2)
                    part = ROWS_AT.index(n)
                    pe.wait_ge(*bank_free(h, "row", part))
                    max_rows(h + 1, part)
                if n % KT == 0:
                    pe.wait_ge(s_qm, 2 * h + half + 1)
                if left < 1 and n >= 3:
                    if n >= len(LAST_BANKS):
                        pe.wait_ge(s_exp, STEPS * h + n - len(LAST_BANKS) + 1)
                elif not (isinstance(h, int) and h == 0 and n < 3):
                    pe.wait_ge(*bank_free(h, "block", n))
                elif n == 1:
                    pe.wait_ge(s_qm, 2)
                nc.tensor.matmul(block_bank(n, left < 1), kstack[b][:, kt * P:(kt + 1) * P],
                                 qstack[b][:, half * HALF:(half + 1) * HALF], start=True, stop=True
                                 ).then_inc(s_st, 1)
                j = n // 2 + FIRST_PAIRS
                if j < PAIRS and left >= 1:
                    pair(h + 1, (b + 1) % RING, j, n % 2, False)
                elif left >= 2:
                    if j == PAIRS and n % 2 == 0:
                        stacked(b + 2, nth)
                    pair(h + 2, (b + 2) % RING, j - PAIRS, n % 2, False)
                if left >= 1 and n >= 5 and n % 4 == 1:
                    weigh(h, b, n // 4 - 1)
                if left < 1 and n >= 8 and n % 4 == 0:
                    weigh(h, b, n // 4 - 2)

        def stacked(b, nth):
            pe.wait_ge(s_stack[b % RING], LOADED * (nth + b // RING - (b % RING == 0)))

        def head(h, b, nth, left):
            steps(h, b, nth, left, STARTED, STEPS)
            if left >= 1:
                b1, nth1 = (b + 1) % RING, nth + (b + 1) // RING
                steps(h + 1, b1, nth1, left - 1, 0, STARTED - 1)
                weigh(h, b, SG - 1)
                steps(h + 1, b1, nth1, left - 1, STARTED - 1, STARTED)
            else:
                weigh(h, b, SG - 2)
                weigh(h, b, SG - 1)

        pe.wait_ge(s_qfirst, len(RUNS) * 16)
        for j in range(PAIRS):
            for u in range(2):
                pair(0, 0, j, u, True)
        pe.wait_ge(s_rl, len(TURNS))
        pe.wait_ge(s_const, 1)
        pe.wait_ge(s_m3, 1)
        for half in range(2):
            max_rows(0, half)
        stacked(1, 1)
        for j in range(FIRST_PAIRS):
            for u in range(2):
                pair(1, 1, j, u, False)
        pe.sem_inc(s_pv, SLOTS)
        pe.sem_inc(s_ot, 1)
        steps(0, 0, 1, 2, 0, STARTED)
        with pe.Fori(0, HEADS // RING - 1) as i:
            for b in range(RING):
                head(RING * i + b, b, i + 1, 2)
        for h in range(HEADS - RING, HEADS):
            head(h, h % RING, h // RING + 1, min(2, HEADS - 1 - h))


def project_and_experts(nc, ctx, oT, keep):
    sb = lambda name, shape, dt: ctx.enter_context(nc.sbuf_tensor(name, shape, dt))
    sem = lambda name: ctx.enter_context(nc.semaphore(name))
    banks = [ctx.enter_context(nc.psum_tensor(f"bank{i}", [P, 2, HALF], F32)) for i in range(4)]
    x, woT, ctxT, mask, ident = (keep[n] for n in ("x", "woT", "ctxT", "mask", "ident"))

    den = sb("den", [P, 4, P], F32)
    rden = sb("rden", [P, P], F32)
    rres = sb("rres", [P, P], F32)
    rpart = sb("rpart", [P, 3, P], BF16)
    rrow = sb("rrow", [3 * HEADS, T], BF16)
    att = sb("att", [P, DC, T], F32)
    stats = sb("stats", [P, QT, 6], F32)
    mv = sb("mv", [P, QT, 2], F32)
    var = sb("var", [P, QT], F32)
    std = sb("std", [P, QT], F32)
    rstd = sb("rstd", [P, QT], F32)
    x1 = sb("x1", [P, QT, D], F32)
    x1T = sb("x1T", [P, DC, T], F32)
    silu = sb("silu", [P, 2, HALF], F32)
    hid = oT[:, 0:E1 * 2, :].rearrange("p (e f) t -> p e f t", f=2)
    xm = oT[:, E1 * 2:E1 * 4, :].rearrange("p (e c) t -> p e c t", c=DC)

    s_den = sem("s_den")
    s_rden = sem("s_rden")
    s_rrow = sem("s_rrow")
    s_u = sem("s_u")
    s_uc = sem("s_uc")
    s_r = sem("s_r")
    s_dch = sem("s_dch")
    s_att = sem("s_att")
    s_proj = sem("s_proj")
    s_sum = sem("s_sum")
    s_var = sem("s_var")
    s_std = sem("s_std")
    s_x1 = sem("s_x1")
    s_tr = sem("s_tr")
    s_x1T = sem("s_x1T")
    s_xm = [sem("s_xmd"), sem("s_xmp")]
    s_z = sem("s_z")
    s_si = sem("s_si")
    s_h = sem("s_h")
    s_y = sem("s_y")
    s_x2 = sem("s_x2")

    block = ctx.enter_context(nc.Block())
    SPREAD = T // P

    HT = QT // 2

    def order_of_z():
        for half in range(2):
            for e in range(E1):
                for f in range(2):
                    yield e, half, f

    @block.sync
    def _(sp):
        for g in range(4):
            sp.dma_start(den[:, g, :], oT[32 * g + HD:32 * g + HD + 1, :, :]).then_inc(s_den, 16)
        sp.wait_ge(s_rden, 1)
        for part in range(3):
            sp.dma_start(rrow[part * HEADS:(part + 1) * HEADS, :].rearrange("h (c t) -> h c t", c=SPREAD),
                         rpart[:, part, :]).then_inc(s_rrow, 16)

    @block.gpsimd
    def _(pool):
        for qt in range(QT):
            pool.wait_ge(s_x1T, qt + 1)
            t = slice(qt * P, (qt + 1) * P)
            for e in (2, 3):
                m = mask[:, e, t].rearrange("p (o t) -> p o t", o=1).broadcast_to([P, DC, P])
                nc.gpsimd.tensor_tensor(xm[:, e, :, t], x1T[:, :, t], m, ALU.mult).then_inc(s_xm[1], 1)
                pool.wait_ge(s_xm[1], 2 * qt + e - 1)

    @block.scalar
    def _(act):
        for c in range(DC):
            act.wait_ge(s_u, c + 1)
            nc.scalar.activation(att[:, c, :], banks[c][:, :, :].rearrange("p a n -> p (a n)"), ACT.Copy
                                 ).then_inc(s_uc, 1)

        def root(nth, half):
            h = slice(half * HT, (half + 1) * HT)
            act.wait_ge(s_var, 2 * nth + half + 1)
            nc.scalar.activation(std[:, h], var[:, h], ACT.Sqrt).then_inc(s_std, 1)

        for half in range(2):
            root(0, half)
        for qt in range(QT):
            act.wait_ge(s_tr, qt + 1)
            nc.scalar.activation(x1T[:, :, qt * P:(qt + 1) * P], banks[2 + qt % 2][:, 0, 0:D]
                                 .rearrange("p (c n) -> p c n", c=DC), ACT.Copy).then_inc(s_x1T, 1)
        for n in range(4 * E1):
            act.wait_ge(s_z, n + 1)
            if n >= 2:
                act.wait_ge(s_h, n - 1)
            nc.scalar.activation(silu[:, n % 2, :], banks[n % 4][:, 0, :], ACT.Silu).then_inc(s_si, 1)
        for half in range(2):
            root(1, half)

    @block.vector
    def _(dve):
        order = [0]

        def link(ins, wait=True):
            order[0] += 1
            ins.then_inc(s_dch, 1)
            if wait:
                dve.wait_ge(s_dch, order[0])

        dve.wait_ge(s_den, 64)
        link(nc.vector.tensor_tensor(den[:, 0:2, :], den[:, 0:2, :], den[:, 2:4, :], ALU.add))
        link(nc.vector.tensor_tensor(den[:, 0, :], den[:, 0, :], den[:, 1, :], ALU.add))
        link(nc.vector.reciprocal(rden[:, :], den[:, 0, :]))
        link(nc.vector.tensor_copy(rpart[:, 0, :], rden[:, :]))
        link(nc.vector.tensor_tensor(rres[:, :], rden[:, :], rpart[:, 0, :], ALU.subtract))
        link(nc.vector.tensor_copy(rpart[:, 1, :], rres[:, :]))
        nc.vector.tensor_tensor(rpart[:, 2, :], rres[:, :], rpart[:, 1, :], ALU.subtract).then_inc(s_rden, 1)
        dve.wait_ge(s_uc, DC)
        for n in range(2 * DC):
            half, c = n // DC, n % DC
            t = slice(half * HALF, (half + 1) * HALF)
            dve.wait_ge(s_r, n + 1)
            nc.vector.tensor_tensor(att[:, c, t], banks[2 + c][:, half, :], att[:, c, t], ALU.mult
                                    ).then_inc(s_att, 1)

        def norm(nth, ready, bank_of, base, out, done):
            for half in range(2):
                tiles = range(half * HT, (half + 1) * HT)
                h = slice(half * HT, (half + 1) * HT)
                for qt in tiles:
                    dve.wait_ge(ready, qt + 1)
                    nc.vector.tensor_tensor(base[:, qt, :], bank_of(qt), base[:, qt, :], ALU.add).then_inc(s_sum, 1)
                    dve.wait_ge(s_sum, nth * QT + qt + 1)
                    link(nc.vector.bn_stats(stats[:, qt, :], base[:, qt, :]), wait=(qt == tiles[-1]))
                for qt in tiles:
                    link(nc.vector.bn_aggr(mv[:, qt, :], stats[:, qt, :]), wait=(qt == tiles[-1]))
                nc.vector.tensor_scalar(var[:, h], mv[:, h, 1], EPS, None, ALU.add).then_inc(s_var, 1)
                dve.wait_ge(s_std, 2 * nth + half + 1)
                link(nc.vector.reciprocal(rstd[:, h], std[:, h]))
                for qt in tiles:
                    nc.vector.tensor_scalar(out[:, qt, :], base[:, qt, :], mv[:, qt, 0:1], rstd[:, qt:qt + 1],
                                            ALU.subtract, ALU.mult).then_inc(done, 1)

        norm(0, s_proj, lambda qt: banks[qt % 2][:, 0, 0:D], x, x1, s_x1)
        for qt in range(QT):
            dve.wait_ge(s_x1T, qt + 1)
            t = slice(qt * P, (qt + 1) * P)
            for e in (0, 1):
                m = mask[:, e, t].rearrange("p (o t) -> p o t", o=1).broadcast_to([P, DC, P])
                nc.vector.tensor_tensor(xm[:, e, :, t], x1T[:, :, t], m, ALU.mult).then_inc(s_xm[0], 1)
        for n, (e, half, f) in enumerate(order_of_z()):
            dve.wait_ge(s_si, n + 1)
            nc.vector.tensor_tensor(hid[:, e, f, half * HALF:(half + 1) * HALF], banks[n % 4][:, 0, :],
                                    silu[:, n % 2, :], ALU.mult).then_inc(s_h, 1)
        dve.wait_ge(s_x1, QT)
        norm(1, s_y, lambda qt: banks[qt % 2][:, 1, 0:D], x1, x, s_x2)

    @block.tensor
    def _(pe):
        for c in range(DC):
            for half in range(2):
                for j in range(2):
                    for q in range(4):
                        last = nc.tensor.matmul(banks[c][32 * q:32 * q + 32, half, :], keep["pick"][:, j, :],
                                                oT[:, 8 * c + 2 * q + j, half * HALF:(half + 1) * HALF],
                                                start=(j == 0), stop=(j == 1), skip_group_check=True)
            last.then_inc(s_u, 1)
        pe.wait_ge(s_rrow, 3 * 16)
        for n in range(2 * DC):
            half, c = n // DC, n % DC
            nc.tensor.matmul(banks[2 + c][:, half, :], keep["spread"][:, 8 * c:8 * c + 8, :]
                             .rearrange("h q m -> h (q m)"), rrow[:, half * HALF:(half + 1) * HALF],
                             start=True, stop=True).then_inc(s_r, 1)
        for qt in range(QT):
            if qt % (QT // 2) == 0:
                pe.wait_ge(s_att, DC * (qt // (QT // 2) + 1))
            if qt >= 2:
                pe.wait_ge(s_sum, qt - 1)
            for c in range(DC):
                last = nc.tensor.matmul(banks[qt % 2][:, 0, 0:D], att[:, c, qt * P:(qt + 1) * P], woT[:, c, :],
                                        start=(c == 0), stop=(c == DC - 1))
            last.then_inc(s_proj, 1)
        for qt in range(QT):
            pe.wait_ge(s_x1, qt + 1)
            if qt >= 2:
                pe.wait_ge(s_x1T, qt - 1)
            for c in range(DC):
                last = nc.tensor.transpose(banks[2 + qt % 2][:, 0, c * P:(c + 1) * P], x1[:, qt, c * P:(c + 1) * P],
                                           ident)
            last.then_inc(s_tr, 1)
        pe.wait_ge(s_x1T, QT)
        for n, (e, half, f) in enumerate(order_of_z()):
            pe.wait_ge(s_xm[e // 2], QT * (half + 1))
            if n >= 4:
                pe.wait_ge(s_h, n - 3)
            for c in range(DC):
                last = nc.tensor.matmul(banks[n % 4][:, 0, :], ctxT[:, e, c, f * P:(f + 1) * P],
                                        xm[:, e, c, half * HALF:(half + 1) * HALF], start=(c == 0), stop=(c == DC - 1))
            last.then_inc(s_z, 1)
        for qt in range(QT):
            if qt % HT == 0:
                pe.wait_ge(s_h, 2 * E1 * (qt // HT + 1))
            if qt >= 2:
                pe.wait_ge(s_sum, QT + qt - 1)
            for e in range(E1):
                for f in range(2):
                    last = nc.tensor.matmul(banks[qt % 2][:, 1, 0:D], hid[:, e, f, qt * P:(qt + 1) * P],
                                            ctxT[:, e, f, :], start=(e == 0 and f == 0), stop=(e == E1 - 1 and f == 1))
            last.then_inc(s_y, 1)


NE, FFN, TOPK = 64, 176, 6
FC = FFN // 2
SF = 2 * FFN
SFC = SF // FC
UNROLL = 4
TILES = -(-((T * TOPK + NE * (P - 1)) // P) // UNROLL) * UNROLL
ALL = TILES + UNROLL
PICKS = QT * TOPK
ROW = D + NE
FP16 = mybir.dt.float16


def mixture(nc, ctx, a, keep, out):
    sb = lambda name, shape, dt: ctx.enter_context(nc.sbuf_tensor(name, shape, dt))
    pb = lambda name, shape: ctx.enter_context(nc.psum_tensor(name, shape, F32))
    sem = lambda name: ctx.enter_context(nc.semaphore(name))
    x2, gateT, swgu, swd, ident, iota, before, upto, onesb, onesf = (keep[n] for n in (
        "x", "gateT", "swgu", "swd", "ident", "iota", "before", "upto", "onesb", "onesf"))

    iota16 = sb("iota16", [P, P], FP16)
    token = sb("token", [P, QT], F32)
    spare = sb("spare", [P, 1], F32)
    zero = sb("zero3", [P, D], F32)
    x2T = sb("x2T", [P, DC, T], F32)
    logits = sb("logits", [P, QT, NE], F32)
    red = sb("red", [P, 4, QT], F32)
    scores = sb("scores", [P, QT, NE], F32)
    top = sb("top", [P, QT, 8], F32)
    topi = sb("topi", [P, QT, 8], U32)
    topf = sb("topf", [P, QT, 8], F32)
    chosen = sb("chosen", [P, TOPK, QT, NE], F32)
    place = sb("place", [P, TOPK, QT, NE], F32)
    anyj = sb("anyj", [P, QT, NE], BF16)
    picked = sb("picked", [P, QT, NE], F32)
    weight = sb("weight", [P, QT, NE], F32)
    filled = sb("filled", [P, NE], I32)
    tilesi = sb("tilesi", [P, NE], I32)
    tiles = sb("tiles", [P, NE], F32)
    ends = sb("ends", [P, NE], F32)
    base = sb("base", [P, NE], F32)
    where = sb("where", [P, QT, NE], F32)
    slotf = sb("slotf", [P, PICKS], F32)
    sloti = sb("sloti", [P, 3, PICKS], I32)
    rowf = sb("rowf", [P, PICKS], FP16)
    tilef = sb("tilef", [P, PICKS], F32)
    is_row = sb("is_row", [P, PICKS, P], FP16)
    is_tile = sb("is_tile", [P, PICKS, ALL], FP16)
    cfill = sb("cfill", [NE, 2], I32)
    ctilef = sb("ctilef", [NE, 1], F32)
    cend = sb("cend", [NE, 1], F32)
    past = sb("past", [NE, ALL], BF16)
    owner = sb("owner", [1, ALL], I32)
    ownerf = sb("ownerf", [P, ALL], F32)
    rounds = sb("rounds", [1, 2], I32)
    found = sb("found", [P, ALL], F32)
    empty = sb("empty", [P, ALL], F32)
    source = sb("source", [P, ALL], I32)
    target = sb("target", [P, ALL], I32)
    src = [sb(f"src{r}", [P, 1], I32) for r in range(UNROLL)]
    dst = [sb(f"dst{r}", [P, 1], I32) for r in range(UNROLL)]
    xg = [sb(f"xg{r}", [P, ROW], F32) for r in range(UNROLL)]
    wgu = [sb(f"wgu{r}", [P, DC * 2 * FFN], F32) for r in range(UNROLL)]
    wd = [sb(f"wd{r}", [FC, 2 * D], F32) for r in range(UNROLL)]
    wsel = [sb(f"wsel{b}", [P, NE], F32) for b in range(2)]
    wcol = [sb(f"wcol{b}", [P, 1], F32) for b in range(2)]
    yt = [sb(f"yt{r}", [P, D], F32) for r in range(UNROLL)]
    xgT = [sb(f"xgT{b}", [P, D], F32) for b in range(2)]
    silu = [sb(f"silu{b}", [P, FFN], F32) for b in range(2)]
    hid = [sb(f"hid{b}", [P, FFN], F32) for b in range(2)]
    hidT = [sb(f"hidT{b}", [FC, 2 * P], F32) for b in range(2)]
    ssilu = [sb(f"ssilu{b}", [P, SF], F32) for b in range(2)]
    sup = [sb(f"sup{b}", [P, SF], F32) for b in range(2)]
    shid = [sb(f"shid{b}", [P, SF], F32) for b in range(2)]
    shidT = sb("shidT", [FC, SFC * P], F32)
    acc = sb("acc", [P, QT, D], F32)
    acc2 = sb("acc2", [P, QT, D], F32)
    stats = sb("stats3", [P, QT, 6], F32)
    mv = sb("mv3", [P, QT, 2], F32)
    var = sb("var3", [P, QT], F32)
    std = sb("std3", [P, QT], F32)
    rstd = sb("rstd3", [P, QT], F32)
    shift = sb("shift", [P, QT // 2], F32)
    A = [pb(f"A{b}", [P, HALF]) for b in range(2)]
    G = [pb(f"G{b}", [P, HALF]) for b in range(2)]
    H = [pb(f"H{b}", [P, HALF]) for b in range(2)]
    Y = [pb(f"Y{b}", [P, HALF]) for b in range(2)]
    count_row, count_col, end_col = A[1][:, 0:NE], A[1][0:NE, NE:NE + 1], A[1][0:NE, NE + 1:NE + 2]
    owner_all, found_at = A[1][:, P:P + ALL], A[1][:, 2 * P:2 * P + ALL]
    SHARED = [(G[0], G[1]), (H[1], A[0])]
    rows = nc.dram_tensor("rows", [T, ROW], F32, kind="Internal").ap()
    sums = [nc.dram_tensor(f"sums{b}", [T + P, D], F32, kind="Internal").ap() for b in range(2)]
    by_tile = lambda m: m.rearrange("(q p) d -> p q d", p=P)

    s_po = sem("m_po")
    s_pc = sem("m_pc")
    s_ch = sem("m_ch")
    s_xd = sem("m_xd")
    s_tr = sem("m_tr")
    s_x2T = sem("m_x2T")
    s_lg = sem("m_lg")
    s_sub = sem("m_sub")
    s_ex = sem("m_ex")
    s_any = sem("m_any")
    s_wt = sem("m_wt")
    s_rank = sem("m_rank")
    s_ct = sem("m_ct")
    s_ce = sem("m_ce")
    s_past = sem("m_past")
    s_ow = sem("m_ow")
    s_row = sem("m_row")
    s_oh = sem("m_oh")
    s_fd = sem("m_fd")
    s_idx = sem("m_idx")
    s_sg = sem("m_sg")
    s_ss = sem("m_ss")
    s_sh = sem("m_sh")
    s_st = sem("m_st")
    s_shT = sem("m_shT")
    s_sy = sem("m_sy")
    s_acc = sem("m_acc")
    s_sum = sem("m_sum")
    s_src = sem("m_src")
    s_dst = sem("m_dst")
    s_xg = [sem(f"m_xg{r}") for r in range(UNROLL)]
    s_w = [sem(f"m_w{r}") for r in range(UNROLL)]
    s_tx = sem("m_tx")
    s_xT = sem("m_xT")
    s_gu = sem("m_gu")
    s_si = sem("m_si")
    s_h = sem("m_h")
    s_th = sem("m_th")
    s_hT = sem("m_hT")
    s_dn = sem("m_dn")
    s_ws = sem("m_ws")
    s_wc = sem("m_wc")
    s_yc = sem("m_yc")
    s_add = [sem(f"m_add{b}") for b in range(2)]
    s_go = sem("m_go")
    s_all = sem("m_all")
    s_back = [sem(f"m_back{b}") for b in range(2)]
    s_pa = sem("m_pa")
    s_var = sem("m_var")
    s_std = sem("m_std")
    s_shift = sem("m_shift")
    s_y = [sem(f"m_y{b}") for b in range(2)]
    s_out = sem("m_out")

    block = ctx.enter_context(nc.Block())
    ROUNDS = TILES // UNROLL
    LEAST = T * TOPK // P // UNROLL
    HT = QT // 2
    SPAN = 4
    assert (ROUNDS - LEAST) % SPAN == 0

    def steps(engine, step):
        engine.wait_ge(s_row, 2)
        used = engine.value_load(rounds[0:1, 1:2], min_val=LEAST, max_val=ROUNDS)
        for r in range(UNROLL):
            step(r, r)
        with engine.Fori(1, LEAST) as i:
            for r in range(UNROLL):
                step(UNROLL * i + r, r)
        with engine.Fori(0, (ROUNDS - LEAST) // SPAN) as span:
            with engine.If(LEAST + SPAN * span < used):
                with engine.Fori(0, SPAN) as j:
                    i = LEAST + SPAN * span + j
                    with engine.If(i < used):
                        for r in range(UNROLL):
                            step(UNROLL * i + r, r)
        return used

    def round_of(n, r):
        return (n - r) // UNROLL + 1

    def added(n, r):
        return 8 * n - (8 * (r % 2) + 16)

    def after(engine, s, value, n, first):
        if not (isinstance(n, int) and n < first):
            engine.wait_ge(s, value)

    @block.sync
    def _(sp):
        sp.dma_start(by_tile(rows[:, 0:D]), x2).then_inc(s_xd, 16)
        sp.dma_start(by_tile(sums[1][0:T, :]), x2).then_inc(s_sum, 16)
        sp.wait_ge(s_pc, 1)
        for b in range(2):
            sp.dma_start(sums[b][T:T + P, :], zero[:, :]).then_inc(s_sum, 16)
        sp.wait_ge(s_wt, 1)
        sp.dma_start(by_tile(rows[:, D:ROW]), weight[:, :, :]).then_inc(s_xd, 16)
        sp.wait_ge(s_row, 2)

        def load_weights(n, r):
            e = sp.value_load(owner[0:1, bass.ds(n, 1)], min_val=0, max_val=NE - 1)
            sp.dma_start(wgu[r][:, :], a["wgu"][bass.ds(e, 1), :, :].rearrange("o p n -> p (o n)")).then_inc(s_w[r], 16)
            sp.dma_start(wd[r][:, :], a["wd"][bass.ds(e, 1), :, :].rearrange("o p n -> p (o n)")).then_inc(s_w[r], 16)

        for r in range(UNROLL):
            load_weights(r, r)
        sp.wait_ge(s_acc, QT)
        sp.dma_start(by_tile(sums[0][0:T, :]), acc[:, :, :]).then_inc(s_sum, 16)

        def step(n, r):
            sp.wait_ge(s_dn, n + 1)
            sp.sem_inc(s_all, 1)
            load_weights(n + UNROLL, r)

        used = steps(sp, step)
        for r in range(UNROLL):
            sp.wait_ge(s_w[r], 32 * (used + 1))
            sp.sem_inc(s_all, 1)
            sp.wait_ge(s_xg[r], 16 * (used + 1))
            sp.sem_inc(s_all, 1)
        for b in range(2):
            sp.wait_ge(s_add[b], 16 * UNROLL // 2 * used)
            sp.sem_inc(s_all, 1)
        for b in range(2):
            q = slice(b * HT, (b + 1) * HT)
            sp.dma_start(acc[:, q, :], by_tile(sums[0][0:T, :])[:, q, :]).then_inc(s_back[b], 16)
            sp.dma_start(acc2[:, q, :], by_tile(sums[1][0:T, :])[:, q, :]).then_inc(s_back[b], 16)
        for b in range(2):
            q = slice(b * HT, (b + 1) * HT)
            sp.wait_ge(s_y[b], HT)
            sp.dma_start(out[:, q, :], acc[:, q, :]).then_inc(s_out, 16)
        sp.wait_ge(s_out, 32)

    @block.gpsimd
    def _(pool):
        order = [0]

        def link(ins):
            order[0] += 1
            ins.then_inc(s_po, 1)
            pool.wait_ge(s_po, order[0])

        link(nc.gpsimd.iota(iota16[:, :], [[1, P]], base=0, channel_multiplier=0, allow_small_or_imprecise_dtypes=True))
        link(nc.gpsimd.iota(token[:, :], [[P, QT]], base=1, channel_multiplier=1, allow_small_or_imprecise_dtypes=True))
        link(nc.gpsimd.iota(spare[:, :], [[0, 1]], base=T + 1, channel_multiplier=1, allow_small_or_imprecise_dtypes=True))
        link(nc.gpsimd.memset(zero[:, :], 0.0))
        pool.sem_inc(s_pc, 1)

        def shared(qt):
            b = qt % 2
            pool.wait_ge(s_ss, 2 * (qt + 1))
            if qt >= 2:
                pool.wait_ge(s_st, qt - 1)
            nc.gpsimd.tensor_tensor(shid[b][:, :], ssilu[b][:, :], sup[b][:, :], ALU.mult).then_inc(s_sh, 1)
            pool.wait_ge(s_sh, qt + 1)

        for qt in range(3):
            shared(qt)
        pool.wait_ge(s_any, 2)
        link(nc.gpsimd.tensor_tensor(picked[:, :, :], scores[:, :, :], anyj[:, :, :], ALU.mult))
        nc.gpsimd.tensor_tensor(weight[:, :, :], picked[:, :, :], red[:, 3, :].rearrange("p (q o) -> p q o", o=1)
                                .broadcast_to([P, QT, NE]), ALU.mult).then_inc(s_wt, 1)
        pool.wait_ge(s_wt, 1)
        for qt in range(3, QT):
            shared(qt)

        def gather(r):
            nc.gpsimd.indirect_dma_start(xg[r][:, :], None, rows, bass.IndirectOffsetOnAxis(ap=src[r][:, :], axis=0)
                                         ).then_inc(s_xg[r], 16)

        pool.wait_ge(s_xd, 32)
        for r in range(UNROLL):
            pool.wait_ge(s_src, r + 1)
            gather(r)
        pool.wait_ge(s_sum, 64)

        def step(n, r):
            pool.wait_ge(s_tx, n + 1)
            pool.wait_ge(s_ws, n + 1)
            pool.wait_ge(s_src, n + UNROLL + 1)
            pool.sem_inc(s_go, 1)
            gather(r)
            pool.wait_ge(s_yc, n + 1)
            pool.wait_ge(s_dst, n + 1)
            after(pool, s_add[r % 2], added(n, r) + 16, n, 2)
            pool.sem_inc(s_go, 1)
            nc.gpsimd.indirect_dma_start(sums[r % 2], bass.IndirectOffsetOnAxis(ap=dst[r][:, :], axis=0), yt[r][:, :], None,
                                         compute_op=ALU.add).then_inc(s_add[r % 2], 16)
        steps(pool, step)
        for b in range(2):
            pool.wait_ge(s_back[b], 32)
            for qt in range(b * HT + HT // 2, (b + 1) * HT):
                nc.gpsimd.tensor_tensor(acc[:, qt, :], acc[:, qt, :], acc2[:, qt, :], ALU.add).then_inc(s_pa, 1)
                pool.wait_ge(s_pa, qt - HT // 2 * (b + 1) + 1)

    @block.scalar
    def _(act):
        for qt in range(QT):
            act.wait_ge(s_tr, qt + 1)
            nc.scalar.activation(x2T[:, :, qt * P:(qt + 1) * P], A[qt % 2][:, 0:D]
                                 .rearrange("p (c n) -> p c n", c=DC), ACT.Copy).then_inc(s_x2T, 1)
        act.wait_ge(s_sub, 1)
        nc.scalar.activation(scores[:, :, :], logits[:, :, :], ACT.Exp).then_inc(s_ex, 1)

        def shared_gate(qt):
            b = qt % 2
            gate, up = SHARED[b]
            act.wait_ge(s_sg, 2 * qt + 1)
            if qt >= 2:
                act.wait_ge(s_sh, qt - 1)
            nc.scalar.activation(ssilu[b][:, :], gate[:, 0:SF], ACT.Silu).then_inc(s_ss, 1)
            act.wait_ge(s_sg, 2 * qt + 2)
            nc.scalar.activation(sup[b][:, :], up[:, 0:SF], ACT.Copy).then_inc(s_ss, 1)

        def put_source(n, r):
            nc.scalar.activation(src[r][:, :], source[:, bass.ds(n, 1)], ACT.Copy).then_inc(s_src, 1)

        shared_gate(0)
        shared_gate(1)
        for qt in range(QT):
            act.wait_ge(s_st, qt + 1)
            if qt >= 1:
                act.wait_ge(s_sy, qt)
            nc.scalar.activation(shidT[:, :], H[0][0:FC, :], ACT.Copy).then_inc(s_shT, 1)
            if qt + 2 < QT:
                shared_gate(qt + 2)
            act.wait_ge(s_sy, qt + 1)
            nc.scalar.activation(acc[:, qt, :], Y[0][:, 0:D], ACT.Copy).then_inc(s_acc, 1)
        act.wait_ge(s_idx, 1)
        for r in range(UNROLL):
            put_source(r, r)

        def put_target(n, r):
            after(act, s_add[r % 2], added(n, r), n, UNROLL)
            nc.scalar.activation(dst[r][:, :], target[:, bass.ds(n, 1)], ACT.Copy).then_inc(s_dst, 1)

        def move(n, b):
            act.wait_ge(s_tx, n + 1)
            after(act, s_gu, n - 1, n, 2)
            nc.scalar.activation(xgT[b][:, :], A[b][:, 0:D], ACT.Copy).then_inc(s_xT, 1)

        def gate(n, b):
            act.wait_ge(s_gu, n + 1)
            after(act, s_h, n - 1, n, 2)
            nc.scalar.activation(silu[b][:, :], G[b][:, 0:FFN], ACT.Silu).then_inc(s_si, 1)

        move(0, 0)
        move(1, 1)
        gate(0, 0)

        def step(n, r):
            gate(n + 1, (r + 1) % 2)
            move(n + 2, r % 2)
            act.wait_ge(s_xg[r], 16 * round_of(n, r))
            put_source(n + UNROLL, r)
            put_target(n, r)

        steps(act, step)
        for b in range(2):
            h = slice(b * HT, (b + 1) * HT)
            act.wait_ge(s_var, b + 1)
            nc.scalar.activation(std[:, h], var[:, h], ACT.Sqrt).then_inc(s_std, 1)
            if b == 0:
                act.wait_ge(s_shift, 1)
                for qt in range(HT):
                    nc.scalar.activation(acc[:, qt, :], acc[:, qt, :], ACT.Identity, scale=rstd[:, qt:qt + 1],
                                         bias=shift[:, qt:qt + 1]).then_inc(s_y[0], 1)

    @block.vector
    def _(dve):
        order = [0]

        def link(ins, wait=True):
            order[0] += 1
            ins.then_inc(s_ch, 1)
            if wait:
                dve.wait_ge(s_ch, order[0])

        spread = lambda v: v.rearrange("p (q o) -> p q o", o=1).broadcast_to([P, QT, NE])
        dve.wait_ge(s_lg, 1)
        lg = Y[1][:, :].rearrange("p (q e) -> p q e", e=NE)
        link(nc.vector.tensor_reduce(red[:, 0, :], lg, AX.X, ALU.max))
        nc.vector.tensor_tensor(logits[:, :, :], lg, spread(red[:, 0, :]), ALU.subtract).then_inc(s_sub, 1)
        dve.wait_ge(s_ex, 1)
        link(nc.vector.tensor_reduce(red[:, 1, :], scores[:, :, :], AX.X, ALU.add))
        link(nc.vector.reciprocal(red[:, 2, :], red[:, 1, :]))
        link(nc.vector.tensor_tensor(scores[:, :, :], scores[:, :, :], spread(red[:, 2, :]), ALU.mult))
        for qt in range(QT):
            link(nc.vector.max(top[:, qt, :], scores[:, qt, :]), wait=(qt == QT - 1))
        for qt in range(QT):
            link(nc.vector.max_index(topi[:, qt, :], top[:, qt, :], scores[:, qt, :]), wait=(qt == QT - 1))
        link(nc.vector.tensor_copy(topf[:, :, :], topi[:, :, :]))
        experts = iota[:, 0:NE].rearrange("p (o e) -> p o e", o=1).broadcast_to([P, QT, NE])
        for j in range(TOPK):
            link(nc.vector.tensor_tensor(chosen[:, j, :, :], experts, spread(topf[:, :, j]), ALU.is_equal),
                 wait=(j == TOPK - 1))
        nc.vector.tensor_reduce(anyj[:, :, :], chosen[:, :, :, :].rearrange("p j q e -> p (q e) j"), AX.X,
                                ALU.max).then_inc(s_any, 1)
        link(nc.vector.tensor_reduce(red[:, 0, :], top[:, :, 0:TOPK], AX.X, ALU.add))
        link(nc.vector.tensor_scalar(red[:, 1, :], red[:, 0, :], 1e-20, None, ALU.add))
        nc.vector.reciprocal(red[:, 3, :], red[:, 1, :]).then_inc(s_any, 1)
        dve.wait_ge(s_rank, 1)
        link(nc.vector.tensor_scalar(filled[:, :], count_row, float(P - 1), None, ALU.add), wait=False)
        link(nc.vector.tensor_scalar(cfill[:, 0:1], count_col, float(P - 1), None, ALU.add))
        link(nc.vector.tensor_scalar(cfill[:, 1:2], cfill[:, 0:1], 7, None, ALU.logical_shift_right))
        nc.vector.tensor_copy(ctilef[:, :], cfill[:, 1:2]).then_inc(s_ct, 1)
        link(nc.vector.tensor_scalar(tilesi[:, :], filled[:, :], 7, None, ALU.logical_shift_right))
        link(nc.vector.tensor_copy(tiles[:, :], tilesi[:, :]))
        link(nc.vector.tensor_tensor_scan(ends[:, :], onesf, tiles[:, :], 0.0, ALU.mult, ALU.add))
        link(nc.vector.tensor_tensor(base[:, :], ends[:, :], tiles[:, :], ALU.subtract))
        link(nc.vector.tensor_scalar(base[:, :], base[:, :], float(P), None, ALU.mult))
        link(nc.vector.tensor_tensor(where[:, :, :], lg, base[:, :].rearrange("p (o e) -> p o e", o=1)
                                     .broadcast_to([P, QT, NE]), ALU.add))
        for j in range(TOPK):
            link(nc.vector.tensor_tensor(place[:, j, :, :], chosen[:, j, :, :], where[:, :, :], ALU.mult),
                 wait=False)
        link(nc.vector.tensor_scalar(rounds[0:1, 0:1], ends[0:1, NE - 1:NE], float(UNROLL - 1), None, ALU.add))
        nc.vector.tensor_scalar(rounds[0:1, 1:2], rounds[0:1, 0:1], 2, None, ALU.logical_shift_right).then_inc(s_row, 1)
        dve.wait_ge(s_ce, 1)
        link(nc.vector.tensor_copy(cend[:, :], end_col))
        nc.vector.tensor_scalar(past[:, :], iota[0:NE, 0:ALL], cend[:, 0:1], None, ALU.is_ge).then_inc(s_past, 1)
        link(nc.vector.tensor_reduce(slotf[:, :], place[:, :, :, :].rearrange("p j q e -> p (j q) e"), AX.X, ALU.add))
        link(nc.vector.tensor_copy(sloti[:, 0, :], slotf[:, :]))
        link(nc.vector.tensor_scalar(sloti[:, 1, :], sloti[:, 0, :], P - 1, None, ALU.bitwise_and), wait=False)
        link(nc.vector.tensor_scalar(sloti[:, 2, :], sloti[:, 0, :], 7, None, ALU.logical_shift_right))
        link(nc.vector.tensor_copy(rowf[:, :], sloti[:, 1, :]), wait=False)
        link(nc.vector.tensor_copy(tilef[:, :], sloti[:, 2, :]))
        dve.wait_ge(s_ow, 1)
        nc.vector.tensor_scalar(owner[:, :], owner_all[0:1, :], float(NE - 1), None, ALU.min).then_inc(s_row, 1)
        link(nc.vector.tensor_scalar(ownerf[:, :], owner_all, float(NE - 1), None, ALU.min), wait=False)
        dve.wait_ge(s_pc, 1)
        for n in range(PICKS):
            if n % QT == 0:
                nc.vector.tensor_tensor(is_row[:, n:n + QT, :],
                                        iota16[:, :].rearrange("p (o r) -> p o r", o=1).broadcast_to([P, QT, P]),
                                        rowf[:, n:n + QT].rearrange("p (n o) -> p n o", o=1).broadcast_to([P, QT, P]),
                                        ALU.is_equal).then_inc(s_oh, 1)
            nc.vector.tensor_scalar(is_tile[:, n, :], iota16[:, 0:ALL], tilef[:, n:n + 1], token[:, n % QT:n % QT + 1],
                                    ALU.is_equal, ALU.mult).then_inc(s_oh, 1)
        dve.wait_ge(s_fd, PICKS)
        link(nc.vector.tensor_copy(found[:, :], found_at))
        link(nc.vector.tensor_scalar(source[:, :], found[:, :], -1.0, 0.0, ALU.add, ALU.max), wait=False)
        link(nc.vector.tensor_scalar(empty[:, :], found[:, :], 0.0, spare[:, 0:1], ALU.is_equal, ALU.mult))
        nc.vector.scalar_tensor_tensor(out=target[:, :], in0=found[:, :], scalar=-1.0, in1=empty[:, :], op0=ALU.add,
                                       op1=ALU.add).then_inc(s_idx, 1)

        def multiply(n, b):
            dve.wait_ge(s_si, n + 1)
            after(dve, s_th, n - 1, n, 2)
            nc.vector.tensor_tensor(hid[b][:, :], G[b][:, FFN:2 * FFN], silu[b][:, :], ALU.mult).then_inc(s_h, 1)

        multiply(0, 0)

        def step(n, r):
            b = r % 2
            dve.wait_ge(s_th, n + 1)
            after(dve, s_dn, n - 1, n, 2)
            nc.vector.tensor_copy(hidT[b][:, :], H[b][0:FC, 0:2 * P]).then_inc(s_hT, 1)
            dve.wait_ge(s_xg[r], 16 * round_of(n, r))
            after(dve, s_yc, n - 1, n, 2)
            nc.vector.scalar_tensor_tensor(out=wsel[b][:, :], in0=iota[:, 0:NE], scalar=ownerf[:, bass.ds(n, 1)],
                                           in1=xg[r][:, D:ROW], op0=ALU.is_equal, op1=ALU.mult).then_inc(s_ws, 1)
            multiply(n + 1, (r + 1) % 2)
            dve.wait_ge(s_ws, n + 1)
            nc.vector.tensor_reduce(wcol[b][:, :], wsel[b][:, :], AX.X, ALU.add).then_inc(s_wc, 1)
            dve.wait_ge(s_wc, n + 1)
            dve.wait_ge(s_dn, n + 1)
            after(dve, s_add[r % 2], added(n, r), n, UNROLL)
            nc.vector.tensor_scalar(yt[r][:, :], Y[b][:, 0:D], wcol[b][:, 0:1], None, ALU.mult).then_inc(s_yc, 1)

        steps(dve, step)
        def sums_of(b):
            dve.wait_ge(s_back[b], 32)
            first = b * HT
            for qt in range(first, first + HT // 2):
                link(nc.vector.tensor_tensor(acc[:, qt, :], acc[:, qt, :], acc2[:, qt, :], ALU.add),
                     wait=(qt == first + HT // 2 - 1))
            for qt in range(first, first + HT):
                if qt == first + HT // 2:
                    dve.wait_ge(s_pa, (b + 1) * HT // 2)
                link(nc.vector.bn_stats(stats[:, qt, :], acc[:, qt, :]), wait=(qt == first + HT - 1))
            for qt in range(first, first + HT):
                link(nc.vector.bn_aggr(mv[:, qt, :], stats[:, qt, :]), wait=(qt == first + HT - 1))
            nc.vector.tensor_scalar(var[:, first:first + HT], mv[:, first:first + HT, 1], EPS, None, ALU.add
                                    ).then_inc(s_var, 1)

        def deviations(b):
            h = slice(b * HT, (b + 1) * HT)
            dve.wait_ge(s_std, b + 1)
            link(nc.vector.reciprocal(rstd[:, h], std[:, h]))

        sums_of(0)
        deviations(0)
        link(nc.vector.tensor_tensor(shift[:, :], mv[:, 0:HT, 0], rstd[:, 0:HT], ALU.mult))
        nc.vector.tensor_scalar(shift[:, :], shift[:, :], -1.0, None, ALU.mult).then_inc(s_shift, 1)
        sums_of(1)
        deviations(1)
        for qt in range(HT, QT):
            nc.vector.tensor_scalar(acc[:, qt, :], acc[:, qt, :], mv[:, qt, 0:1], rstd[:, qt:qt + 1], ALU.subtract,
                                    ALU.mult).then_inc(s_y[1], 1)

    @block.tensor
    def _(pe):
        for qt in range(QT + 2):
            if qt >= 2:
                pe.wait_ge(s_x2T, qt - 1)
            if qt < QT:
                for c in range(DC):
                    last = nc.tensor.transpose(A[qt % 2][:, c * P:(c + 1) * P], x2[:, qt, c * P:(c + 1) * P], ident)
                last.then_inc(s_tr, 1)
            if qt >= 2:
                t = qt - 2
                for c in range(DC):
                    last = nc.tensor.matmul(Y[1][:, t * NE:(t + 1) * NE], x2T[:, c, t * P:(t + 1) * P],
                                            gateT[:, c, :], start=(c == 0), stop=(c == DC - 1))
        last.then_inc(s_lg, 1)

        def shared_gate(qt):
            if qt >= 2:
                pe.wait_ge(s_ss, 2 * (qt - 1))
            for w in range(2):
                for c in range(DC):
                    last = nc.tensor.matmul(SHARED[qt % 2][w][:, 0:SF], x2T[:, c, qt * P:(qt + 1) * P],
                                            swgu[:, c, w * SF:(w + 1) * SF], start=(c == 0), stop=(c == DC - 1))
                last.then_inc(s_sg, 1)

        def shared_turn(qt):
            pe.wait_ge(s_sh, qt + 1)
            if qt >= 1:
                pe.wait_ge(s_shT, qt)
            for f in range(SFC):
                last = nc.tensor.transpose(H[0][0:FC, f * P:(f + 1) * P], shid[qt % 2][:, f * FC:(f + 1) * FC], ident)
            last.then_inc(s_st, 1)

        def shared_down(qt):
            if qt >= 1:
                pe.wait_ge(s_acc, qt)
            pe.wait_ge(s_shT, qt + 1)
            for f in range(SFC):
                last = nc.tensor.matmul(Y[0][:, 0:D], shidT[:, f * P:(f + 1) * P], swd[:, f, :],
                                        start=(f == 0), stop=(f == SFC - 1))
            last.then_inc(s_sy, 1)

        def ranks():
            pe.wait_ge(s_any, 1)
            for qt in range(QT):
                for s in range(qt + 1):
                    nc.tensor.matmul(Y[1][:, qt * NE:(qt + 1) * NE], before if s == qt else onesb, anyj[:, s, :],
                                     start=(s == 0), stop=(s == qt))
            for s in range(QT):
                nc.tensor.matmul(count_row, onesb, anyj[:, s, :], start=(s == 0), stop=(s == QT - 1))
            for s in range(QT):
                last = nc.tensor.matmul(count_col, anyj[:, s, :], onesb[:, 0:1], start=(s == 0), stop=(s == QT - 1))
            last.then_inc(s_rank, 1)

        def find(n):
            pe.wait_ge(s_oh, n // QT + 1 + n + 1)
            nc.tensor.matmul(found_at, is_row[:, n, :], is_tile[:, n, :], start=(n == 0), stop=(n == PICKS - 1)
                             ).then_inc(s_fd, 1)

        SOUGHT = {QT - 3: (0, 2), QT - 2: (2, 3), QT - 1: (3, TOPK)}
        shared_gate(0)
        shared_gate(1)
        for qt in range(QT):
            shared_turn(qt)
            if qt + 2 < QT:
                shared_gate(qt + 2)
            if qt == 1:
                ranks()
            if qt == 2:
                pe.wait_ge(s_ct, 1)
                nc.tensor.matmul(end_col, upto, ctilef[:, :], start=True, stop=True).then_inc(s_ce, 1)
            shared_down(qt)
            if qt == 2:
                pe.wait_ge(s_past, 1)
                nc.tensor.matmul(owner_all, onesb[0:NE, :], past[:, :], start=True, stop=True).then_inc(s_ow, 1)
            for n in range(*(QT * j for j in SOUGHT.get(qt, (0, 0)))):
                find(n)
        pe.wait_ge(s_acc, QT)
        pe.wait_ge(s_idx, 1)

        def turn_rows(n, r, b):
            pe.wait_ge(s_xg[r], 16 * round_of(n, r))
            after(pe, s_xT, n - 1, n, 2)
            for c in range(DC):
                last = nc.tensor.transpose(A[b][:, c * P:(c + 1) * P], xg[r][:, c * P:(c + 1) * P], ident)
            last.then_inc(s_tx, 1)

        def gate_up(n, r, b):
            pe.wait_ge(s_w[r], 32 * round_of(n, r))
            pe.wait_ge(s_xT, n + 1)
            after(pe, s_h, n - 1, n, 2)
            for c in range(DC):
                last = nc.tensor.matmul(G[b][:, 0:2 * FFN], xgT[b][:, c * P:(c + 1) * P],
                                        wgu[r][:, c * 2 * FFN:(c + 1) * 2 * FFN], start=(c == 0), stop=(c == DC - 1))
            last.then_inc(s_gu, 1)

        turn_rows(0, 0, 0)
        turn_rows(1, 1, 1)
        gate_up(0, 0, 0)

        def step(n, r):
            b = r % 2
            pe.wait_ge(s_h, n + 1)
            after(pe, s_hT, n - 1, n, 2)
            for f in range(2):
                last = nc.tensor.transpose(H[b][0:FC, f * P:(f + 1) * P], hid[b][:, f * FC:(f + 1) * FC], ident)
            last.then_inc(s_th, 1)
            r1, r2 = (r + 1) % UNROLL, (r + 2) % UNROLL
            gate_up(n + 1, r1, (r + 1) % 2)
            turn_rows(n + 2, r2, b)
            pe.wait_ge(s_hT, n + 1)
            after(pe, s_yc, n - 1, n, 2)
            for f in range(2):
                last = nc.tensor.matmul(Y[b][:, 0:D], hidT[b][:, f * P:(f + 1) * P], wd[r][:, f * D:(f + 1) * D],
                                        start=(f == 0), stop=(f == 1))
            last.then_inc(s_dn, 1)

        steps(pe, step)


def program(nc, a, out):
    with ExitStack() as whole:
        def kept(name, shape, dt=F32):
            t = whole.enter_context(nc.sbuf_tensor(name, shape, dt))
            return t[tuple(slice(None) for _ in shape)]

        keep = {
            "x": kept("x", [P, QT, D]),
            "woT": kept("woT", [P, DC, D]),
            "ctxT": kept("ctxT", [P, E1, DC, F1]),
            "mask": kept("mask", [P, E1, T], BF16),
            "ident": kept("ident", [P, P]),
            "pick": kept("pick", [P, 2, 32]),
            "spread": kept("spread", [3 * HEADS, HEADS, HD], BF16),
            "gateT": kept("gateT", [P, DC, NE]),
            "swgu": kept("swgu", [P, DC, 2 * SF]),
            "swd": kept("swd", [FC, SFC, D]),
            "iota": kept("iota", [P, P]),
            "before": kept("before", [P, P], BF16),
            "upto": kept("upto", [NE, NE]),
            "onesb": kept("onesb", [P, P], BF16),
            "onesf": kept("onesf", [P, NE]),
            "s_ld": whole.enter_context(nc.semaphore("s_ld")),
        }
        with nc.sbuf_tensor("oT", [P, HEADS, T], F32) as oT:
            with ExitStack() as ctx:
                attention(nc, ctx, a, oT, keep)
            with ExitStack() as ctx:
                project_and_experts(nc, ctx, oT, keep)
        with ExitStack() as ctx:
            mixture(nc, ctx, a, keep, out)


def kernel(x, itok_BxS_13_99985, ctx_2048, L0_attn_kv_k, L0_attn_kv_v, L0_attn_Wq, L0_attn_Wo, L0_ffn_gate_w,
           L0_ffn_w_gate_up, L0_ffn_w_down, L0_ffn_ws_gate_up, L0_ffn_ws_down):
    import concourse.bacc as bacc
    from concourse.bass_utils import run_bass_kernel_spmd as run

    chunks = lambda m: np.ascontiguousarray(m.reshape(-1, P, m.shape[1]).transpose(1, 0, 2))
    xs = np.asarray(x).reshape(T, D)
    arrays = {
        "x": chunks(xs),
        "xT": chunks(xs.T),
        "wqT": chunks(np.asarray(L0_attn_Wq).T),
        "woT": chunks(np.asarray(L0_attn_Wo).T),
        "kT": chunks(np.asarray(L0_attn_kv_k).reshape(KV, D).T),
        "v": np.ascontiguousarray(np.asarray(L0_attn_kv_v).reshape(KT, P, HEADS, HD).transpose(2, 1, 0, 3)
                                  .reshape(HEADS, P, KT * HD)),
        "ids": np.ascontiguousarray(np.asarray(itok_BxS_13_99985).reshape(T)),
        "ctxT": np.ascontiguousarray(np.asarray(ctx_2048).transpose(0, 2, 1).reshape(E1, DC, P, F1)
                                     .transpose(2, 0, 1, 3)),
    }
    rows = lambda m, p: np.ascontiguousarray(m.transpose(0, 2, 1).reshape(m.shape[0], -1, p, m.shape[1])
                                             .transpose(0, 2, 1, 3))
    arrays["wgu"] = rows(np.asarray(L0_ffn_w_gate_up), P).reshape(NE, P, DC * 2 * FFN)
    arrays["wd"] = rows(np.asarray(L0_ffn_w_down), FC).reshape(NE, FC, 2 * D)
    arrays["swgu"] = rows(np.asarray(L0_ffn_ws_gate_up)[None], P)[0]
    arrays["swd"] = rows(np.asarray(L0_ffn_ws_down)[None], FC)[0]
    arrays["gateT"] = chunks(np.asarray(L0_ffn_gate_w).T)
    nc = bacc.Bacc("TRN2", target_bir_lowering=False, num_devices=1)
    a = {n: nc.dram_tensor(n + "_in", v.shape, mybir.dt.from_np(v.dtype), kind="ExternalInput").ap()
         for n, v in arrays.items()}
    out = nc.dram_tensor("out", (P, QT, D), F32, kind="ExternalOutput").ap()
    program(nc, a, out)
    r = run(nc, [{n + "_in": v for n, v in arrays.items()}], core_ids=[0])
    return np.ascontiguousarray(r.results[0]["out"].transpose(1, 0, 2)).reshape(4, 256, D)
```
